# Optimizing a Trainium2 kernel written in Bass

```python
import numpy as np
import jax
import jax.numpy as jnp

def _softmax(x, axis=-1):
    return jax.nn.softmax(x, axis=axis)

def _gelu(x):
    return jax.nn.gelu(x, approximate=True)

def _silu(x):
    return jax.nn.silu(x)

def _sigmoid(x):
    return jax.nn.sigmoid(x)

def _layernorm(x, axis=-1, eps=1e-05):
    m = jnp.mean(x, axis=axis, keepdims=True)
    v = jnp.var(x, axis=axis, keepdims=True)
    return (x - m) / jnp.sqrt(v + eps)

def _scatter_add(tgt, idx, src, axis=0):
    return tgt.at[idx].add(src)

def _segment_sum(src, seg, n):
    return jax.ops.segment_sum(src, seg, n)
kernel_name = 'mk_gnn_resnorm_d2_gnn_r64_8f3bf7'

def setup_inputs(seed: int=0):
    np.random.seed(seed)
    _w = jnp.asarray

    def _rec_inputs():
        import jax
        import jax.numpy as jnp
        _gk = jax.random.key(seed)
        x = -0.0005121 + 1.001 * jax.random.normal(jax.random.fold_in(_gk, 1), (100000, 32), jnp.float32)
        src = jax.random.randint(jax.random.fold_in(_gk, 2), (25000,), 0, 100000, jnp.int32)
        dst = jax.random.randint(jax.random.fold_in(_gk, 3), (25000,), 0, 100000, jnp.int32)
        _o = jnp.argsort(dst, stable=True)
        src = src[_o]
        dst = dst[_o]
        edge_attr_4 = 0.000398945 + 1.00003 * jax.random.normal(jax.random.fold_in(_gk, 11), (25000, 4), jnp.float32)
        edge_weight = jax.random.uniform(jax.random.fold_in(_gk, 13), (25000,), jnp.float32, 0.0, 1)
        return (x, src, dst, edge_attr_4, edge_weight)
    x, src, dst, edge_attr_4, edge_weight = _rec_inputs()

    def _L0_gnn_setup():
        import jax, jax.numpy as jnp
        import numpy as np
        N_NODES = 100000
        N_EDGES = 25000
        IN_DIM = 32
        HID = 64
        OUT_DIM = 32
        EDGE_DIM = 4
        key = jax.random.key(seed)
        ks = jax.random.split(key, 12)
        x = jax.random.normal(ks[0], (N_NODES, IN_DIM), dtype=jnp.float32)
        edge_index = jax.random.randint(ks[1], (2, N_EDGES), 0, N_NODES, dtype=jnp.int32)
        edge_attr = jax.random.normal(ks[2], (N_EDGES, EDGE_DIM), dtype=jnp.float32)

        def lin(k, fan_in, fan_out):
            kw, kb = jax.random.split(k)
            bound = 1.0 / np.sqrt(fan_in)
            W = jax.random.uniform(kw, (fan_in, fan_out), minval=-bound, maxval=bound, dtype=jnp.float32)
            b = jax.random.uniform(kb, (fan_out,), minval=-bound, maxval=bound, dtype=jnp.float32)
            return (W, b)
        W1, b1 = lin(ks[3], 2 * IN_DIM, HID)
        W2, b2 = lin(ks[4], HID, 2 * HID)
        W3, b3 = lin(ks[5], 2 * HID, HID)
        W4, b4 = lin(ks[6], HID, OUT_DIM)
        return {'x': x, 'edge_index': edge_index, 'edge_attr': edge_attr, 'W1': W1, 'b1': b1, 'W2': W2, 'b2': b2, 'W3': W3, 'b3': b3, 'W4': W4, 'b4': b4}
    _L0_gnn_all = _L0_gnn_setup()
    _L0_gnn_in = {k: v for k, v in _L0_gnn_all.items() if k in ('W1', 'b1', 'W2', 'b2', 'W3', 'b3', 'W4', 'b4')}
    del _L0_gnn_all

    def _L1_gnn_setup():
        import jax, jax.numpy as jnp
        import numpy as np
        N_NODES = 100000
        N_EDGES = 50000
        D_IN = 32
        D_OUT = 32
        K = 3
        key = jax.random.key(seed)
        k1, k2, k3, k4 = jax.random.split(key, 4)
        x = jax.random.normal(k1, (N_NODES, D_IN), dtype=jnp.float32)
        edge_index = jax.random.randint(k2, (2, N_EDGES), 0, N_NODES, dtype=jnp.int32)
        edge_weight = jax.random.uniform(k3, (N_EDGES,), dtype=jnp.float32)
        W = jax.random.normal(k4, (K, D_IN, D_OUT), dtype=jnp.float32) * 0.1
        b = jnp.zeros((D_OUT,), dtype=jnp.float32)
        return {'x': x, 'edge_index': edge_index, 'edge_weight': edge_weight, 'W': W, 'b': b}
    _L1_gnn_all = _L1_gnn_setup()
    _L1_gnn_in = {k: v for k, v in _L1_gnn_all.items() if k in ('W', 'b')}
    del _L1_gnn_all
    return {'x': x, 'src': src, 'dst': dst, 'edge_attr_4': edge_attr_4, 'edge_weight': edge_weight, 'L0_gnn_W1': _L0_gnn_in['W1'], 'L0_gnn_b1': _L0_gnn_in['b1'], 'L0_gnn_W2': _L0_gnn_in['W2'], 'L0_gnn_b2': _L0_gnn_in['b2'], 'L0_gnn_W3': _L0_gnn_in['W3'], 'L0_gnn_b3': _L0_gnn_in['b3'], 'L0_gnn_W4': _L0_gnn_in['W4'], 'L0_gnn_b4': _L0_gnn_in['b4'], 'L1_gnn_W': _L1_gnn_in['W'], 'L1_gnn_b': _L1_gnn_in['b']}

def reference(x, src, dst, edge_attr_4, edge_weight, L0_gnn_W1, L0_gnn_b1, L0_gnn_W2, L0_gnn_b2, L0_gnn_W3, L0_gnn_b3, L0_gnn_W4, L0_gnn_b4, L1_gnn_W, L1_gnn_b):
    import jax
    import jax.numpy as jnp

    def _L0_gnn_ref(x, edge_index, edge_attr, W1, b1, W2, b2, W3, b3, W4, b4):
        import jax, jax.numpy as jnp
        import numpy as np
        N_NODES = 100000
        N_EDGES = 25000
        IN_DIM = 32
        HID = 64
        OUT_DIM = 32
        EDGE_DIM = 4
        j_idx = edge_index[0]
        i_idx = edge_index[1]
        x_j = x[j_idx]
        x_i = x[i_idx]
        msg = jnp.concatenate([x_i, x_j - x_i], axis=-1)
        h = jax.nn.relu(msg @ W1 + b1)
        h = jax.nn.relu(h @ W2 + b2)
        h = jax.nn.relu(h @ W3 + b3)
        m = h @ W4 + b4
        s = jax.ops.segment_sum(m, i_idx, num_segments=N_NODES)
        cnt = jax.ops.segment_sum(jnp.ones((m.shape[0],), m.dtype), i_idx, num_segments=N_NODES)
        return s / jnp.maximum(cnt, 1.0)[:, None]

    def _L1_gnn_ref(x, edge_index, edge_weight, W, b):
        import jax, jax.numpy as jnp
        import numpy as np
        N_NODES = 100000
        N_EDGES = 50000
        D_IN = 32
        D_OUT = 32
        K = 3
        src, dst = (edge_index[0], edge_index[1])
        n = x.shape[0]
        deg = jax.ops.segment_sum(edge_weight, dst, num_segments=n)
        dinv = jnp.where(deg > 0, jax.lax.rsqrt(jnp.maximum(deg, 1e-12)), 0.0)
        w_hat = -dinv[dst] * edge_weight * dinv[src]

        def prop(v):
            return jax.ops.segment_sum(w_hat[:, None] * v[src], dst, num_segments=n)
        Tx0 = x
        Tx1 = prop(Tx0)
        out = Tx0 @ W[0] + Tx1 @ W[1]
        Tx2 = 2.0 * prop(Tx1) - Tx0
        out = out + Tx2 @ W[2]
        out = out + b
        return jax.nn.relu(out)
    edge_index = jnp.stack([src, dst])
    x = _layernorm(x + _L0_gnn_ref(x, edge_index, edge_attr_4, L0_gnn_W1, L0_gnn_b1, L0_gnn_W2, L0_gnn_b2, L0_gnn_W3, L0_gnn_b3, L0_gnn_W4, L0_gnn_b4), axis=-1)
    x = _layernorm(x + _L1_gnn_ref(x, edge_index, edge_weight, L1_gnn_W, L1_gnn_b), axis=-1)
    return x

_drawn_inputs = setup_inputs


def setup_inputs(seed=0):
    import zlib

    import numpy as np

    out = dict(_drawn_inputs(seed))
    spreads = {'L1_gnn_b': (0.0, 0.1)}
    factors = {'L0_gnn_W1': 4.203,
     'L0_gnn_b1': 8.0,
     'L0_gnn_W2': 3.705,
     'L0_gnn_b2': 8.0,
     'L0_gnn_W3': 3.205,
     'L0_gnn_b3': 5.2,
     'L0_gnn_b4': 4.045}
    for name, (base, spread) in spreads.items():
        noise = np.random.default_rng([zlib.crc32(name.encode()), seed]).standard_normal(out[name].shape)
        drawn = base * np.exp(spread * noise) if base else spread * noise
        out[name] = jnp.asarray(drawn.astype(out[name].dtype))
    for name, factor in factors.items():
        out[name] = (out[name] * factor).astype(out[name].dtype)
    return out
```

```python
from contextlib import ExitStack

import concourse.bass as bass
from concourse import mybir

ALU = mybir.AluOpType
ACT = mybir.ActivationFunctionType
AX = mybir.AxisListType.X
F32 = mybir.dt.float32
I32 = mybir.dt.int32

P = 128
BIG = 1 << 20
EPS = 1e-5
OFF = 2


def build(nc, x, src, dst, edge_weight, W1, b1, W2, b2, W3, b3, W4, b4, Wc, bc, out):
    N, D = x.shape
    E = src.shape[0]
    H1, H2, H3 = W1.shape[1], W2.shape[1], W3.shape[1]
    C = 14
    T = -(-E // (P * 2 * C)) * 2 * C
    LOOPS = T // (2 * C)
    FULL, REM = E // T, E % T
    PAIRS = [4, 3]
    UNITS = C // 2
    C2 = 2 * C
    R = 60
    NK = 13
    TAILP, TAILR = 40, 4
    assert P * R * NK + TAILP * TAILR == N and 2 * D == H1 and sum(PAIRS) == UNITS
    BANKS = [4, 4, 4, 3]
    FBANKS = [4, 4, 4, 2]
    RT32 = float(D) ** 0.5

    ctx = ExitStack()
    with ctx:
        def sb(name, shape, dt=F32):
            return ctx.enter_context(nc.sbuf_tensor(name, shape, dt))

        def sem(name):
            return ctx.enter_context(nc.semaphore(name))

        dst_x = sb("dst_x", [P, T + 2], I32)
        dst_up = sb("dst_up", [P, T], I32)
        src_i = sb("src_i", [P, T], I32)
        w = sb("w", [P, T])
        dst1 = sb("dst1", [P, T + 2])
        src1 = sb("src1", [P, T])
        d_first = sb("d_first", [P, P])
        d_delta = sb("d_delta", [P, T])
        cont = sb("cont", [P, T])
        last = sb("last", [P, T])
        pre = sb("pre", [P, T])
        cnt = sb("cnt", [P, T])
        rcnt = sb("rcnt", [P, T])
        prer = sb("prer", [P, T])
        deg = sb("deg", [P, T])
        dinv = sb("dinv", [P, T])
        ndinv = sb("ndinv", [P, T])
        ndinv2 = sb("ndinv2", [P, T])
        n2dinv = sb("n2dinv", [P, T])
        above = sb("above", [P, T])
        below = sb("below", [P, T])
        same = sb("same", [P, T])
        w_eff = sb("w_eff", [P, T])
        tmp = sb("tmp", [P, T])
        hits = sb("hits", [P, 4, T])
        ones = sb("ones", [P, T])
        epsc = sb("epsc", [P, 1])
        zeros = sb("zeros", [P, T])
        slot_i = sb("slot_i", [P, T], I32)
        scat_i = sb("scat_i", [P, T], I32)
        X1 = sb("X1", [P, T, D])
        S = sb("S", [P, T + 1, D])
        T1 = sb("T1", [P, T, D])
        x_ring = sb("x_ring", [P, 2, C, 2 * D])
        y_ring = sb("y_ring", [P, 2, C, D])
        o_ring = sb("o_ring", [P, 2, C, D])
        di_ring = sb("di_ring", [P, 2, C], I32)
        si_ring = sb("si_ring", [P, 2, C], I32)
        mk = sb("mk", [P, D, C + 1])
        sc_in = sb("sc_in", [P, D, C + 1])
        sc_out = sb("sc_out", [P, D, C + 1])
        corr = sb("corr", [P, C2, D])
        xT = sb("xT", [P, 512])
        h1 = sb("h1", [P, 512])
        h2 = sb("h2", [P, 2, 512])
        h3 = sb("h3", [P, 512])
        le = sb("le", [P, 2, 2, P])
        leT = sb("leT", [P, 2, 2 * P])
        w1s = sb("w1s", [P, P])
        w1b = sb("w1b", [P, P])
        w2s = sb("w2s", [P, 2, H2])
        w3s = sb("w3s", [P, 2, P])
        w4s = sb("w4s", [P, 2 * D])
        b1c = sb("b1c", [P, 1])
        b2c = sb("b2c", [P, 1])
        b3c = sb("b3c", [P, 1])
        b4r = sb("b4r", [P, D])
        ident = sb("ident", [P, P])
        wd = sb("wd", [P, P])
        wd2 = sb("wd2", [P, P])
        wf = sb("wf", [P, D])
        wf2 = sb("wf2", [D, D])
        brow = sb("brow", [1, 512])
        onerow = sb("onerow", [1, P])
        tails = sb("tails", [P, D])
        spans = sb("spans", [P, D])
        tailT = sb("tailT", [D, P])
        spanT = sb("spanT", [D, P])
        carT = sb("carT", [D, P])
        car = sb("car", [P, D])
        xin = sb("xin", [P, R, D])
        x1d = sb("x1d", [P, R, D])
        sqd = sb("sqd", [P, R, D])
        rd = sb("rd", [P, R, D])
        od = sb("od", [P, R, D])
        x1T = sb("x1T", [P, 2, 512])
        st = sb("st", [P, 8, R])
        Z = sb("Z", [P, C, 4 * D])
        ZT = sb("ZT", [P, 2, 512])
        sqf = sb("sqf", [P, C2, D])

        bank = [ctx.enter_context(nc.psum_tensor(f"bank{i}", [P, 512], F32)) for i in range(8)]
        xT_ps, h1_ps, h3_ps, m_ps, leT_ps, dq_ps = (bank[i] for i in (0, 1, 4, 5, 6, 7))
        h2_ps = [bank[2], bank[3]]
        car_ps = bank[6]
        x1T_ps = [bank[0], bank[1]]
        hd_ps = [bank[2], bank[3]]
        ZT_ps = [bank[4], bank[5]]
        hf_ps = bank[7]

        y1_dram = nc.dram_tensor("y1_by_slot", [P * T, D], F32, kind="Internal").ap()
        y2_dram = nc.dram_tensor("y2_by_slot", [P * T, D], F32, kind="Internal").ap()

        s_edges = sem("s_edges")
        s_wts = sem("s_wts")
        s_gx = [sem(f"s_gx{i}") for i in range(2)]
        s_gy = [sem(f"s_gy{i}") for i in range(2)]
        s_sc = [sem(f"s_sc{i}") for i in range(2)]
        s_y1 = sem("s_y1")
        s_y2 = sem("s_y2")
        s_xin = sem("s_xin")
        s_od = sem("s_od")
        o_od = sem("o_od")
        o_sc = sem("o_sc")
        p_id = sem("p_id")
        p_idx = sem("p_idx")
        p_begun = sem("p_begun")
        v_fill = sem("v_fill")
        v_deg = sem("v_deg")
        v_ss = sem("v_ss")
        v_dss = sem("v_dss")
        v_dss2 = sem("v_dss2")
        v_fss = sem("v_fss")
        v_pad = sem("v_pad")
        v_wts = sem("v_wts")
        v_diag = sem("v_diag")
        v_tail = sem("v_tail")
        v_ct = sem("v_ct")
        v_le = sem("v_le")
        v_cnt = sem("v_cnt")
        v_m = sem("v_m")
        v_slot = sem("v_slot")
        v_y = sem("v_y")
        v_xc = sem("v_xc")
        v_y1 = sem("v_y1")
        v_y2 = sem("v_y2")
        v_scat = sem("v_scat")
        v_dxc = sem("v_dxc")
        v_dx1 = sem("v_dx1")
        v_dh = sem("v_dh")
        v_dxc2 = sem("v_dxc2")
        v_od = sem("v_od")
        v_z = sem("v_z")
        v_fh = sem("v_fh")
        v_fxc = sem("v_fxc")
        v_o = sem("v_o")
        v_step = sem("v_step")
        t_d0 = sem("t_d0")
        t_tail = sem("t_tail")
        t_ct = sem("t_ct")
        t_leT = sem("t_leT")
        t_dq = sem("t_dq")
        t_xT = sem("t_xT")
        t_h1 = sem("t_h1")
        t_h2 = sem("t_h2")
        t_h3 = sem("t_h3")
        t_m = sem("t_m")
        t_dT = sem("t_dT")
        t_dh = sem("t_dh")
        t_ZT = sem("t_ZT")
        t_hf = sem("t_hf")
        a_deg = sem("a_deg")
        a_sd = sem("a_sd")
        a_dsd = sem("a_dsd")
        a_dsd2 = sem("a_dsd2")
        a_fsd = sem("a_fsd")
        a_leT = sem("a_leT")
        a_xT = sem("a_xT")
        a_h1 = sem("a_h1")
        a_h2 = sem("a_h2")
        a_h3 = sem("a_h3")
        a_xd = sem("a_xd")
        a_sq = sem("a_sq")
        a_dsq = sem("a_dsq")
        a_dT = sem("a_dT")
        a_dsq2 = sem("a_dsq2")
        a_z = sem("a_z")
        a_ZT = sem("a_ZT")
        a_fsq = sem("a_fsq")

        def need(eng, s, n):
            eng.wait_ge(s, n + OFF)

        def over_f(a, n):
            return a.rearrange("p (n o) -> p n o", o=1).broadcast_to([a.shape[0], n, D])

        def over_t(a, n):
            return a.rearrange("p (o f) -> p o f", o=1).broadcast_to([a.shape[0], n, D])

        y1_st = y1_dram.rearrange("(p t) f -> p t f", p=P)
        y2_st = y2_dram.rearrange("(p t) f -> p t f", p=P)
        x_d = x[0:P * R * NK, :].rearrange("(p r) f -> p r f", p=P)
        out_d = out[0:P * R * NK, :].rearrange("(p r) f -> p r f", p=P)
        x_tail = x[P * R * NK:N, :].rearrange("(p r) f -> p r f", r=TAILR)
        out_tail = out[P * R * NK:N, :].rearrange("(p r) f -> p r f", r=TAILR)

        EDGE_DMAS = 9
        WT_DMAS = 32
        block = ctx.enter_context(nc.Block())

        @block.sync
        def _(sp):
            def edge_rows(a, s0, p0, n, m):
                return a[s0:s0 + n * T].rearrange("(p t) -> p t", t=T)[:, 0:m] if n > 1 else \
                    a[s0:s0 + m].rearrange("(p t) -> p t", p=1)

            sp.sem_inc(o_od, OFF)
            sp.sem_inc(o_sc, OFF)
            sp.wait_ge(v_pad, 4)
            sp.dma_start(dst_x[0:FULL, 1:T + 1], edge_rows(dst, 0, 0, FULL, T)).then_inc(s_edges, 16)
            sp.dma_start(dst_x[FULL:P, 1:REM + 1], edge_rows(dst, FULL * T, 0, 1, REM)).then_inc(s_edges, 16)
            sp.dma_start(src_i[0:FULL, :], edge_rows(src, 0, 0, FULL, T)).then_inc(s_edges, 16)
            sp.dma_start(src_i[FULL:P, 0:REM], edge_rows(src, FULL * T, 0, 1, REM)).then_inc(s_edges, 16)
            sp.dma_start(w[0:FULL, :], edge_rows(edge_weight, 0, 0, FULL, T)).then_inc(s_edges, 16)
            sp.dma_start(w[FULL:P, 0:REM], edge_rows(edge_weight, FULL * T, 0, 1, REM)).then_inc(s_edges, 16)
            sp.dma_start(dst_up[1:P, :], edge_rows(dst, 0, 0, FULL, T)).then_inc(s_edges, 16)
            with nc.allow_non_contiguous_dma(reason="one neighbour for each partition"):
                sp.dma_start(dst_x[1:P, 0:1], edge_rows(dst, 0, 0, FULL, T)[:, T - 1:T]).then_inc(s_edges, 16)
                sp.dma_start(dst_x[0:FULL - 1, T + 1:T + 2],
                             edge_rows(dst, T, 0, FULL - 1, T)[:, 0:1]).then_inc(s_edges, 16)

            sp.wait_ge(v_fill, 8)

            def wt(o, i):
                sp.dma_start(o, i).then_inc(s_wts, 16)

            for g in range(2):
                h = g * H1
                wt(w1s[h:h + D, h:h + H1], W1[0:D, :])
                wt(w1s[h + D:h + 2 * D, h:h + H1], W1[D:2 * D, :])
                wt(w1b[h:h + D, h:h + H1], W1[D:2 * D, :])
                wt(w2s[h:h + H1, g, :], W2[:, :])
                wt(w3s[:, g, h:h + H3], W3[:, :])
                wt(w4s[h:h + H3, g * D:(g + 1) * D], W4[:, :])
                wt(b1c[h:h + H1, :], b1.rearrange("(p o) -> p o", o=1))
                wt(b3c[h:h + H3, :], b3.rearrange("(p o) -> p o", o=1))
            wt(b2c[:, :], b2.rearrange("(p o) -> p o", o=1))
            wt(b4r[:, :], b4.rearrange("(o f) -> o f", o=1).broadcast_to([P, D]))
            for g in range(4):
                h = g * D
                wt(wd[h:h + D, h:h + D], Wc[0])
                wt(wd2[h:h + D, h:h + D], Wc[2])
            wt(wf[0:D, :], Wc[0])
            wt(wf2[:, :], Wc[2])
            wt(wf[D:2 * D, :], Wc[1])
            wt(wf[2 * D:3 * D, :], Wc[2])
            wt(wf[3 * D:3 * D + 1, :], bc.rearrange("(o f) -> o f", o=1))
            wt(brow.rearrange("o (r f) -> o r f", f=D),
               bc.rearrange("(o r f) -> o r f", o=1, r=1).broadcast_to([1, 512 // D, D]))

            sp.dma_start(xin[:, :, :], x_d[:, 0:R, :]).then_inc(s_xin, 16)
            with sp.Fori(0, LOOPS) as i:
                need(sp, v_y1, i + 1)
                sp.dma_start(y1_st[:, bass.ds(i * C2, C2), :], T1[:, bass.ds(i * C2, C2), :]).then_inc(s_y1, 16)

            def dense_io(k):
                need(sp, v_dxc, k + 1)
                sp.dma_start(xin[:, :, :], x_d[:, bass.ds(k * R + R, R), :]).then_inc(s_xin, 16)
                need(sp, v_od, k + 1)
                sp.dma_start(out_d[:, bass.ds(k * R, R), :], od[:, :, :]).then_inc(s_od, 16)
                sp.wait_ge(s_od, (k + 1) * 16)
                sp.sem_inc(o_od)

            with sp.Fori(0, LOOPS) as k:
                dense_io(k)
            with sp.Fori(0, LOOPS) as i:
                need(sp, v_y2, i + 1)
                sp.dma_start(y2_st[:, bass.ds(i * C2, C2), :], S[:, bass.ds(i * C2 + 1, C2), :]).then_inc(s_y2, 16)
            with sp.Fori(LOOPS, NK - 1) as k:
                dense_io(k)
            need(sp, v_dxc, NK)
            sp.dma_start(xin[0:TAILP, 0:TAILR, :], x_tail).then_inc(s_xin, 16)
            need(sp, v_od, NK)
            sp.dma_start(out_d[:, (NK - 1) * R:NK * R, :], od[:, :, :]).then_inc(s_od, 16)
            sp.wait_ge(s_od, 16 * NK)
            sp.sem_inc(o_od)
            need(sp, v_od, NK + 1)
            sp.dma_start(out_tail, od[0:TAILP, 0:TAILR, :]).then_inc(s_od, 16)
            sp.wait_ge(s_od, 16 * (NK + 1))

            with sp.Fori(0, LOOPS) as i:
                for s in range(2):
                    sp.wait_ge(s_sc[s], (i + 1) * (16 * C))
                    sp.sem_inc(o_sc)

        @block.gpsimd
        def _(pool):
            pool.sem_inc(p_idx, OFF)
            top_node = pool.to_reg(N - 1)
            top_slot = pool.to_reg(P * T - 1)
            nc.gpsimd.memset(ident[:, :], 0.0).then_inc(p_id, 1)
            pool.wait_ge(p_id, 1)
            nc.gpsimd.affine_select(out=ident[:, :], in_=ident[:, :], compare_op=ALU.not_equal, fill=1.0,
                                    base=0, pattern=[[-1, P]], channel_multiplier=1).then_inc(p_id, 1)

            def rows(s, ring, table, idx, k, top, done):
                nc.gpsimd.indirect_dma_start(
                    out=ring, out_offset=None, in_=table,
                    in_offset=bass.IndirectOffsetOnAxis(ap=idx[:, s, k:k + 1], axis=0),
                    bounds_check=top, oob_is_err=False).then_inc(done, 16)

            pool.wait_ge(s_edges, 16 * EDGE_DMAS)
            pool.wait_ge(v_fill, 8)
            with pool.Fori(0, LOOPS) as i:
                for s in range(2):
                    c = i * 2 + s
                    need(pool, a_xd, c - 1)
                    nc.gpsimd.tensor_copy(di_ring[:, s, :], dst_x[:, bass.ds(c * C + 1, C)]).then_inc(p_idx, 1)
                    nc.gpsimd.tensor_copy(si_ring[:, s, :], src_i[:, bass.ds(c * C, C)]).then_inc(p_idx, 1)
                    need(pool, p_idx, c * 2 + 2)
                    pool.sem_inc(p_begun)
                    for k in range(C):
                        rows(s, x_ring[:, s, k, 0:D], x[:, :], di_ring, k, top_node, s_gx[s])
                        rows(s, x_ring[:, s, k, D:2 * D], x[:, :], si_ring, k, top_node, s_gx[s])

            pool.wait_ge(v_slot, 1)
            for stage, (stored, table) in enumerate(((s_y1, y1_dram), (s_y2, y2_dram))):
                pool.wait_ge(stored, 16 * LOOPS)
                with pool.Fori(0, LOOPS) as i:
                    for s in range(2):
                        c = i * 2 + s + stage * 2 * LOOPS
                        need(pool, v_y, c - 1)
                        nc.gpsimd.tensor_copy(si_ring[:, s, :], slot_i[:, bass.ds((i * 2 + s) * C, C)]).then_inc(p_idx, 1)
                        need(pool, p_idx, c + 4 * LOOPS + 1)
                        pool.sem_inc(p_begun)
                        for k in range(C):
                            rows(s, y_ring[:, s, k, :], table[:, :], si_ring, k, top_slot, s_gy[s])

            pool.wait_ge(s_od, 16 * (NK + 1))
            with pool.Fori(0, LOOPS) as i:
                for s in range(2):
                    c = i * 2 + s
                    need(pool, o_sc, c - 1)
                    nc.gpsimd.tensor_copy(di_ring[:, s, :], scat_i[:, bass.ds(c * C, C)]).then_inc(p_idx, 1)
                    need(pool, p_idx, c + 8 * LOOPS + 1)
                    need(pool, v_o, c + 1)
                    pool.sem_inc(p_begun)
                    for k in range(C):
                        nc.gpsimd.indirect_dma_start(
                            out=out[:, :], out_offset=bass.IndirectOffsetOnAxis(ap=di_ring[:, s, k:k + 1], axis=0),
                            in_=o_ring[:, s, k, :], in_offset=None,
                            bounds_check=top_node, oob_is_err=False).then_inc(s_sc[s], 16)
            for s in range(2):
                pool.wait_ge(s_sc[s], 16 * C * LOOPS)

        @block.tensor
        def _(pe):
            for q in (t_leT, t_dq, t_xT, t_h1, t_h2, t_h3, t_m, t_dT, t_dh, t_ZT, t_hf):
                pe.sem_inc(q, OFF)
            pe.wait_ge(p_id, 2)

            def carry(k):
                pe.wait_ge(v_tail, k + 1)
                ins = pe.transpose(car_ps[0:D, 0:P], tails[:, :], ident[:, :])
                if k == 0:
                    ins = pe.transpose(car_ps[0:D, P:2 * P], spans[:, :], ident[:, :])
                ins.then_inc(t_tail, 1)
                pe.wait_ge(v_ct, k + 1)
                pe.transpose(car_ps[:, 2 * P:2 * P + D], carT[:, :], ident[0:D, 0:D]).then_inc(t_ct, 1)

            pe.wait_ge(v_diag, 1)
            pe.matmul(dq_ps[:, 0:P], ones[:, 0:P], leT[:, 0, 0:P], start=True, stop=True).then_inc(t_d0, 1)
            carry(0)
            pe.wait_ge(v_wts, 1)

            def look_T(c, u, s):
                U, b = c * UNITS + u, (s + u) % 2
                need(pe, v_le, U + 1)
                need(pe, a_leT, U)
                for j in range(2):
                    ins = pe.transpose(leT_ps[:, j * P:(j + 1) * P], le[:, b, j, :], ident[:, :])
                ins.then_inc(t_leT, 1)

            def look_D(c, u, s):
                U, b = c * UNITS + u, (s + u) % 2
                need(pe, a_leT, U + 1)
                need(pe, v_cnt, U)
                for j in range(2):
                    ins = pe.matmul(dq_ps[:, j * T:(j + 1) * T], leT[:, b, j * P:(j + 1) * P], d_delta[:, :],
                                    start=True, stop=True)
                ins.then_inc(t_dq, 1)

            def mlp_T(i, c, v, s):
                if v == 0:
                    pe.wait_ge(s_gx[s], (i + 1) * (32 * C))
                need(pe, a_xT, c * 2 + v)
                for q in range(PAIRS[v]):
                    t = 2 * (q + v * PAIRS[0])
                    ins = pe.transpose(xT_ps[:, q * P:(q + 1) * P],
                                       x_ring[:, s, t:t + 2, :].rearrange("p a b -> p (a b)"), ident[:, :])
                ins.then_inc(t_xT, 1)

            def mlp_1(c, v):
                n = PAIRS[v] * P
                need(pe, a_xT, c * 2 + v + 1)
                need(pe, a_h1, c * 2 + v)
                pe.matmul(h1_ps[:, 0:n], w1s[:, :], xT[:, 0:n], start=True, stop=True).then_inc(t_h1, 1)

            def mlp_2(c, v):
                n = PAIRS[v] * P
                need(pe, a_h1, c * 2 + v + 1)
                for g in range(2):
                    need(pe, a_h2, c * 4 + 2 * v + g - 1)
                    pe.matmul(h2_ps[g][:, 0:n], w2s[:, g, :], h1[:, 0:n], start=True, stop=True).then_inc(t_h2, 1)

            def mlp_3(c, v):
                n = PAIRS[v] * P
                need(pe, a_h2, c * 4 + 2 * v + 2)
                need(pe, a_h3, c * 2 + v)
                for g in range(2):
                    ins = pe.matmul(h3_ps[:, 0:n], w3s[:, g, :], h2[:, g, 0:n], start=(g == 0), stop=(g == 1))
                ins.then_inc(t_h3, 1)

            def mlp_4(c, v):
                need(pe, a_h3, c * 2 + v + 1)
                if v == 0:
                    need(pe, v_m, c)
                for q in range(PAIRS[v]):
                    g = q + v * PAIRS[0]
                    ins = pe.matmul(m_ps[:, g * 2 * D:(g + 1) * 2 * D], h3[:, q * P:(q + 1) * P], w4s[:, :],
                                    start=True, stop=True)
                ins.then_inc(t_m, 1)

            with pe.Fori(0, LOOPS) as i:
                for s in range(2):
                    c = i * 2 + s
                    look_T(c, 0, s)
                    mlp = [lambda: mlp_T(i, c, 0, s), lambda: mlp_1(c, 0), lambda: mlp_2(c, 0),
                           lambda: mlp_3(c, 0), lambda: (mlp_4(c, 0), mlp_T(i, c, 1, s)),
                           lambda: mlp_1(c, 1), lambda: mlp_2(c, 1)]
                    for u in range(UNITS):
                        if u + 1 < UNITS:
                            look_T(c, u + 1, s)
                        mlp[u]()
                        look_D(c, u, s)
                    mlp_3(c, 1)
                    mlp_4(c, 1)
            carry(1)

            def dense(k, banks, pn, w0):
                def turn(b):
                    need(pe, a_dT, w0 + b - 1)
                    for g in range(banks[b]):
                        r = 4 * (g + sum(banks[0:b]))
                        ins = pe.transpose(x1T_ps[b % 2][:, g * P:g * P + pn],
                                           x1d[0:pn, r:r + 4, :].rearrange("p a b -> p (a b)"),
                                           ident[0:pn, 0:pn])
                    ins.then_inc(t_dT, 1)

                need(pe, v_dx1, k + 1)
                turn(0)
                for b in range(len(banks)):
                    if b + 1 < len(banks):
                        turn(b + 1)
                    n = banks[b]
                    need(pe, a_dT, w0 + b + 1)
                    need(pe, v_dh, w0 + b - 1)
                    pe.matmul(hd_ps[b % 2][0:pn, 0:n * P], onerow[:, 0:pn], brow[:, 0:n * P], start=True, stop=False,
                              skip_group_check=True)
                    for g in range(n):
                        ins = pe.matmul(hd_ps[b % 2][0:pn, g * P:(g + 1) * P], x1T[:, b % 2, g * P:g * P + pn],
                                        wd[:, :], start=False, stop=(g == n - 1), skip_group_check=True)
                    ins.then_inc(t_dh, 1)

            with pe.Fori(0, LOOPS) as k:
                dense(k, BANKS, P, k * 4)
            carry(2)
            with pe.Fori(LOOPS, NK) as k:
                dense(k, BANKS, P, k * 4)
            dense(NK, [1], TAILP, NK * 4)
            carry(3)

            with pe.Fori(0, LOOPS) as i:
                for s in range(2):
                    c = i * 2 + s
                    need(pe, v_z, c + 1)
                    need(pe, a_z, c + 1)
                    need(pe, v_fh, c)
                    def turn(b):
                        need(pe, a_ZT, c * 4 + b - 1)
                        for g in range(FBANKS[b]):
                            ins = pe.transpose(ZT_ps[b % 2][:, g * P:(g + 1) * P], Z[:, g + 4 * b, :], ident[:, :])
                        ins.then_inc(t_ZT, 1)
                    turn(0)
                    for b in range(4):
                        if b < 3:
                            turn(b + 1)
                        need(pe, a_ZT, c * 4 + b + 1)
                        for g in range(FBANKS[b]):
                            t = g + 4 * b
                            ins = pe.matmul(hf_ps[:, t * D:(t + 1) * D], ZT[:, b % 2, g * P:(g + 1) * P], wf[:, :],
                                            start=True, stop=True)
                        ins.then_inc(t_hf, 1)

        @block.scalar
        def _(act):
            for q in (a_leT, a_xT, a_h1, a_h2, a_h3, a_xd, a_sq, a_dsq, a_dT, a_dsq2, a_z, a_ZT, a_fsq,
                      a_sd, a_dsd, a_dsd2, a_fsd):
                act.sem_inc(q, OFF)
            act.wait_ge(v_deg, 1)
            nc.scalar.activation(dinv[:, :], dinv[:, :], ACT.Sqrt).then_inc(a_deg, 1)
            act.wait_ge(s_wts, 16 * WT_DMAS)
            act.wait_ge(v_fill, 9)

            def deviation(ss, n, pn=P):
                return nc.scalar.activation(st[0:pn, ss, 0:n], st[0:pn, ss, 0:n], ACT.Sqrt, bias=epsc[0:pn, 0:1])

            def look(c, u, s):
                U, b = c * UNITS + u, (s + u) % 2
                need(act, t_leT, U + 1)
                need(act, t_dq, U - 1)
                nc.scalar.copy(leT[:, b, :], leT_ps[:, 0:2 * P]).then_inc(a_leT, 1)

            def x_T(c, v):
                n = PAIRS[v] * P
                need(act, t_xT, c * 2 + v + 1)
                need(act, t_h1, c * 2 + v)
                nc.scalar.copy(xT[:, 0:n], xT_ps[:, 0:n]).then_inc(a_xT, 1)

            def relu_1(c, v):
                n = PAIRS[v] * P
                need(act, t_h1, c * 2 + v + 1)
                need(act, t_h2, c * 4 + 2 * v)
                nc.scalar.activation(h1[:, 0:n], h1_ps[:, 0:n], ACT.Relu, bias=b1c[:, 0:1]).then_inc(a_h1, 1)

            def relu_2(c, v):
                n = PAIRS[v] * P
                need(act, t_h3, c * 2 + v)
                for g in range(2):
                    need(act, t_h2, c * 4 + 2 * v + g + 1)
                    nc.scalar.activation(h2[:, g, 0:n], h2_ps[g][:, 0:n], ACT.Relu, bias=b2c[:, 0:1]).then_inc(a_h2, 1)

            def relu_3(c, v):
                n = PAIRS[v] * P
                need(act, t_h3, c * 2 + v + 1)
                need(act, t_m, c * 2 + v)
                nc.scalar.activation(h3[:, 0:n], h3_ps[:, 0:n], ACT.Relu, bias=b3c[:, 0:1]).then_inc(a_h3, 1)

            with act.Fori(0, LOOPS) as i:
                for s in range(2):
                    c = i * 2 + s
                    mlp = [lambda: x_T(c, 0), lambda: relu_1(c, 0), lambda: relu_2(c, 0), lambda: relu_3(c, 0),
                           lambda: x_T(c, 1), lambda: relu_1(c, 1), lambda: relu_2(c, 1)]
                    look(c, 0, s)
                    for u in range(UNITS):
                        if u + 1 < UNITS:
                            look(c, u + 1, s)
                        mlp[u]()
                        if u == 4:
                            nc.scalar.copy(X1[:, bass.ds(c * C, C), :], x_ring[:, s, :, 0:D]).then_inc(a_xd, 1)
                    relu_3(c, 1)

            with act.Fori(0, LOOPS) as i:
                need(act, v_xc, i + 1)
                nc.scalar.activation(sqf[:, :, :], X1[:, bass.ds(i * C2, C2), :], ACT.Square).then_inc(a_sq, 1)
                need(act, v_ss, i + 1)
                deviation(1, C2).then_inc(a_sd, 1)

            def dense(k, banks, pn, rn, w0):
                need(act, v_dxc, k + 1)
                nc.scalar.activation(sqd[0:pn, 0:rn, :], x1d[0:pn, 0:rn, :], ACT.Square).then_inc(a_dsq, 1)
                need(act, v_dss, k + 1)
                deviation(4, rn, pn).then_inc(a_dsd, 1)
                for b, n in enumerate(banks):
                    need(act, t_dT, w0 + b + 1)
                    need(act, t_dh, w0 + b - 1)
                    src_ap = x1T_ps[b % 2][:, 0:n * P] if pn == P else x1T_ps[b % 2][:, 0:pn]
                    dst_ap = x1T[:, b % 2, 0:n * P] if pn == P else x1T[:, b % 2, 0:pn]
                    nc.scalar.copy(dst_ap, src_ap).then_inc(a_dT, 1)
                need(act, v_dxc2, k + 1)
                nc.scalar.activation(sqd[0:pn, 0:rn, :], rd[0:pn, 0:rn, :], ACT.Square).then_inc(a_dsq2, 1)
                need(act, v_dss2, k + 1)
                deviation(4, rn, pn).then_inc(a_dsd2, 1)

            with act.Fori(0, NK) as k:
                dense(k, BANKS, P, R, k * 4)
            dense(NK, [1], TAILP, TAILR, NK * 4)

            act.wait_ge(v_ct, 4)
            with act.Fori(0, LOOPS) as i:
                for s in range(2):
                    c = i * 2 + s
                    need(act, t_ZT, c * 4)
                    nc.scalar.copy(Z[:, :, 0:D], X1[:, bass.ds(c * C, C), :]).then_inc(a_z, 1)
                    for b, n in enumerate(FBANKS):
                        need(act, t_ZT, c * 4 + b + 1)
                        need(act, t_hf, c * 4 + b - 1)
                        nc.scalar.copy(ZT[:, b % 2, 0:n * P], ZT_ps[b % 2][:, 0:n * P]).then_inc(a_ZT, 1)
                    need(act, v_fxc, c + 1)
                    nc.scalar.activation(sqf[:, 0:C, :], corr[:, 0:C, :], ACT.Square).then_inc(a_fsq, 1)
                    need(act, v_fss, c + 1)
                    deviation(7, C).then_inc(a_fsd, 1)

        @block.vector
        def _(dve):
            for q in (v_le, v_cnt, v_m, v_y, v_xc, v_y1, v_y2, v_dxc, v_dx1, v_dh, v_dxc2, v_od, v_z,
                      v_fh, v_fxc, v_o, v_step, v_ss, v_dss, v_dss2, v_fss):
                dve.sem_inc(q, OFF)

            class Steps:

                def __init__(self, base):
                    self.base, self.n = base, 0

                def done(self, ins):
                    self.n += 1
                    ins.then_inc(v_step, 1)

                def seen(self):
                    need(dve, v_step, self.base + self.n)

                def link(self, ins):
                    self.done(ins)
                    self.seen()

            at = Steps(0)
            link = at.link

            dve.memset(dst_x[:, :], BIG).then_inc(v_pad, 1)
            dve.memset(src_i[:, :], BIG).then_inc(v_pad, 1)
            dve.memset(w[:, :], 0.0).then_inc(v_pad, 1)
            dve.memset(dst_up[:, :], -1).then_inc(v_pad, 1)
            dve.memset(x_ring[:, :, :, :], 0.0)
            dve.memset(w1s[:, :], 0.0).then_inc(v_fill, 1)
            dve.memset(w1b[:, :], 0.0).then_inc(v_fill, 1)
            dve.memset(w2s[:, :, :], 0.0).then_inc(v_fill, 1)
            dve.memset(w3s[:, :, :], 0.0).then_inc(v_fill, 1)
            dve.memset(w4s[:, :], 0.0).then_inc(v_fill, 1)
            dve.memset(wd[:, :], 0.0).then_inc(v_fill, 1)
            dve.memset(wd2[:, :], 0.0).then_inc(v_fill, 1)
            dve.memset(wf[:, :], 0.0).then_inc(v_fill, 1)
            dve.memset(epsc[:, :], D * EPS).then_inc(v_fill, 1)
            dve.memset(y_ring[:, :, :, :], 0.0)
            dve.memset(ones[:, :], 1.0)
            dve.memset(zeros[:, :], 0.0)
            dve.memset(onerow[:, :], 1.0)
            dve.memset(S[:, 0:1, :], 0.0)
            dve.memset(mk[:, :, :], 0.0)
            dve.memset(carT[:, :], 0.0)
            dve.memset(tails[:, :], 0.0)
            link(dve.memset(Z[:, :, :], 0.0))
            link(dve.memset(Z[:, :, 3 * D:3 * D + 1], 1.0))

            dve.wait_ge(s_edges, 16 * EDGE_DMAS)
            dve.tensor_scalar(dst1[:, :], dst_x[:, :], 1.0, None, ALU.add)
            dve.tensor_scalar(src1[:, :], src_i[:, :], 1.0, None, ALU.add)
            link(dve.tensor_scalar(tmp[:, :], dst_up[:, :], 1.0, None, ALU.add))
            dve.wait_ge(p_id, 2)
            dve.tensor_scalar(leT[:, 0, 0:P], ident[:, :], dst1[:, 1:2], None, ALU.mult).then_inc(v_diag, 1)
            dve.tensor_tensor(d_delta[:, :], dst1[:, 1:T + 1], tmp[:, :], ALU.subtract)
            dve.tensor_tensor(cont[:, :], dst1[:, 0:T], dst1[:, 1:T + 1], ALU.is_equal)
            link(dve.tensor_tensor(last[:, :], dst1[:, 1:T + 1], dst1[:, 2:T + 2], ALU.not_equal))
            link(dve.tensor_scalar(tmp[:, :], dst1[:, 1:T + 1], float(BIG - 1), None, ALU.add))
            dve.scalar_tensor_tensor(out=scat_i[:, :], in0=last[:, :], scalar=-float(BIG), in1=tmp[:, :],
                                     op0=ALU.mult, op1=ALU.add).then_inc(v_scat, 1)
            dve.tensor_tensor_scan(pre[:, :], cont[:, :], zeros[:, :], 1.0, ALU.mult, ALU.add)
            dve.tensor_tensor_scan(cnt[:, :], cont[:, :], ones[:, :], 0.0, ALU.mult, ALU.add)
            link(dve.tensor_tensor_scan(deg[:, :], cont[:, :], w[:, :], 0.0, ALU.mult, ALU.add))

            def carry(k, at):
                if k == 0:
                    dve.tensor_copy(tails[:, 0:1], cnt[:, T - 1:T])
                    dve.tensor_copy(tails[:, 1:2], deg[:, T - 1:T])
                    dve.tensor_copy(spans[:, :], pre[:, T - 1:T].broadcast_to([P, D])).then_inc(v_tail, 1)
                else:
                    dve.tensor_copy(tails[:, :], S[:, T, :]).then_inc(v_tail, 1)
                dve.wait_ge(t_tail, k + 1)
                if k == 0:
                    at.done(dve.tensor_copy(spanT[:, :], car_ps[0:D, P:2 * P]))
                at.link(dve.tensor_copy(tailT[:, :], car_ps[0:D, 0:P]))
                dve.tensor_tensor_scan(carT[:, 1:P], spanT[:, 0:P - 1], tailT[:, 0:P - 1], 0.0,
                                       ALU.mult, ALU.add).then_inc(v_ct, 1)
                dve.wait_ge(t_ct, k + 1)
                at.link(dve.tensor_copy(car[:, :], car_ps[:, 2 * P:2 * P + D]))

            dve.wait_ge(t_d0, 1)
            link(dve.tensor_copy(d_first[:, :], dq_ps[:, 0:P]))
            carry(0, at)
            dve.scalar_tensor_tensor(out=cnt[:, :], in0=pre[:, :], scalar=car[:, 0:1], in1=cnt[:, :],
                                     op0=ALU.mult, op1=ALU.add)
            link(dve.scalar_tensor_tensor(out=deg[:, :], in0=pre[:, :], scalar=car[:, 1:2], in1=deg[:, :],
                                          op0=ALU.mult, op1=ALU.add))
            dve.reciprocal(rcnt[:, :], cnt[:, :])
            dve.tensor_scalar(dinv[:, :], deg[:, :], 1e-12, None, ALU.max).then_inc(v_deg, 1)
            dve.tensor_scalar(tmp[:, :], deg[:, :], 0.0, None, ALU.is_gt)
            dve.wait_ge(a_deg, 1)
            link(dve.reciprocal(dinv[:, :], dinv[:, :]))
            dve.tensor_tensor(prer[:, :], pre[:, :], rcnt[:, :], ALU.mult)
            link(dve.tensor_tensor(dinv[:, :], dinv[:, :], tmp[:, :], ALU.mult))
            dve.tensor_scalar(ndinv[:, :], dinv[:, :], -1.0, None, ALU.mult)
            dve.tensor_scalar(n2dinv[:, :], dinv[:, :], -2.0, None, ALU.mult)
            link(dve.scalar_tensor_tensor(out=ndinv2[:, :], in0=dinv[:, :], scalar=-1.0, in1=dinv[:, :],
                                          op0=ALU.mult, op1=ALU.mult))

            dve.wait_ge(s_wts, 16 * WT_DMAS)
            dve.tensor_tensor(w1s[:, :], w1s[:, :], w1b[:, :], ALU.subtract)
            dve.tensor_tensor(wd[:, :], wd[:, :], wd2[:, :], ALU.subtract)
            dve.tensor_tensor(wf[0:D, :], wf[0:D, :], wf2[:, :], ALU.subtract).then_inc(v_wts, 1)

            def compare(c, u, s):
                U, b = c * UNITS + u, (s + u) % 2
                need(dve, t_leT, U - 1)
                for j in range(2):
                    t = c * C + (2 * u + j)
                    ins = dve.tensor_scalar(le[:, b, j, :], d_first[:, :], src1[:, bass.ds(t, 1)], 0.0,
                                            ALU.is_le, ALU.add, accum_out=above[:, bass.ds(t, 1)])
                ins.then_inc(v_le, 1)

            def count(c, u):
                U = c * UNITS + u
                need(dve, t_dq, U + 1)
                need(dve, v_cnt, U)
                for j in range(2):
                    t = c * C + (2 * u + j)
                    dve.tensor_scalar(hits[:, 2 * j, :], dq_ps[:, j * T:(j + 1) * T], src1[:, bass.ds(t, 1)], 0.0,
                                      ALU.is_le, ALU.add, accum_out=below[:, bass.ds(t, 1)])
                    ins = dve.tensor_scalar(hits[:, 2 * j + 1, :], dq_ps[:, j * T:(j + 1) * T], src1[:, bass.ds(t, 1)], 0.0,
                                            ALU.is_equal, ALU.add, accum_out=same[:, bass.ds(t, 1)])
                ins.then_inc(v_cnt, 1)

            def scan(at, c):
                t0 = c * C
                dve.tensor_copy(sc_in[:, :, 0], S[:, bass.ds(t0, 1), :].rearrange("p o f -> p (o f)"))
                at.link(dve.tensor_copy(
                    mk[:, :, 1:C + 1],
                    cont[:, bass.ds(t0, C)].rearrange("p (o t) -> p o t", o=1).broadcast_to([P, D, C])))
                at.link(dve.tensor_tensor_scan(sc_out.rearrange("p f t -> p (f t)"),
                                               mk.rearrange("p f t -> p (f t)"),
                                               sc_in.rearrange("p f t -> p (f t)"), 0.0, ALU.mult, ALU.add))
                at.link(dve.tensor_copy(S[:, bass.ds(t0 + 1, C), :],
                                        sc_out[:, :, 1:C + 1].rearrange("p f t -> p t f")))

            base_A, K_A = at.n, 10
            with dve.Fori(0, LOOPS) as i:
                at = Steps(i * K_A + base_A)
                for s in range(2):
                    c = i * 2 + s
                    compare(c, 0, s)
                    for u in range(UNITS):
                        if u + 1 < UNITS:
                            compare(c, u + 1, s)
                        count(c, u)
                    need(dve, t_m, c * 2 + 2)
                    dve.tensor_tensor(sc_in[:, :, 1:C + 1],
                                      m_ps[:, 0:C * D].rearrange("p (t f) -> p f t", f=D),
                                      b4r[:, :].rearrange("p (f o) -> p f o", o=1).broadcast_to([P, D, C]),
                                      ALU.add).then_inc(v_m, 1)
                    scan(at, c)
                    Sc = S[:, bass.ds(c * C + 1, C), :]
                    Xc = X1[:, bass.ds(c * C, C), :]
                    at.link(dve.tensor_tensor(corr[:, 0:C, :], Sc, over_f(rcnt[:, bass.ds(c * C, C)], C), ALU.mult))
                    need(dve, a_xd, c + 1)
                    at.done(dve.tensor_tensor(Xc, Xc, corr[:, 0:C, :], ALU.add))
                assert at.n == K_A, at.n
            end_A = base_A + K_A * LOOPS
            at = Steps(end_A)
            at.seen()
            at.done(dve.tensor_scalar(tmp[:, :], same[:, :], 0.0, None, ALU.is_gt))
            at.link(dve.scalar_tensor_tensor(out=below[:, :], in0=above[:, :], scalar=float(T), in1=below[:, :],
                                             op0=ALU.mult, op1=ALU.add))
            at.done(dve.tensor_tensor(w_eff[:, :], w[:, :], tmp[:, :], ALU.mult))
            at.link(dve.tensor_scalar(below[:, :], below[:, :], float(BIG - T - 1), None, ALU.add))
            dve.scalar_tensor_tensor(out=slot_i[:, :], in0=tmp[:, :], scalar=-float(BIG), in1=below[:, :],
                                     op0=ALU.mult, op1=ALU.add).then_inc(v_slot, 1)
            carry(1, at)

            def norm_sum(at, rows, k, n, pn=P):
                at.link(dve.tensor_reduce(st[0:pn, k, 0:n], rows, AX, ALU.add))

            def centre(o, rows, k, n, pn=P):
                return dve.scalar_tensor_tensor(out=o, in0=over_f(st[0:pn, k, 0:n], n), scalar=-1.0 / D, in1=rows,
                                                op0=ALU.mult, op1=ALU.add)

            def norm_squares(sq, k, n, pn=P):
                return dve.tensor_reduce(st[0:pn, k, 0:n], sq, AX, ALU.add)

            def scaled(o, rows, k, n, pn=P):
                return dve.scalar_tensor_tensor(out=o, in0=rows, scalar=RT32, in1=over_f(st[0:pn, k, 0:n], n),
                                                op0=ALU.mult, op1=ALU.mult)

            def invert(at, k, n, pn=P):
                at.link(dve.reciprocal(st[0:pn, k, 0:n], st[0:pn, k, 0:n]))

            base, K_A2 = end_A + at.n, 5
            with dve.Fori(0, LOOPS) as i:
                at = Steps(i * K_A2 + base)
                cols = bass.ds(i * C2, C2)
                Xc = X1[:, cols, :]
                at.link(dve.tensor_tensor(corr[:, :, :], over_f(prer[:, cols], C2), over_t(car[:, :], C2), ALU.mult))
                at.link(dve.tensor_tensor(corr[:, :, :], Xc, corr[:, :, :], ALU.add))
                norm_sum(at, corr[:, :, :], 0, C2)
                centre(Xc, corr[:, :, :], 0, C2).then_inc(v_xc, 1)
                need(dve, a_sq, i + 1)
                norm_squares(sqf[:, :, :], 1, C2).then_inc(v_ss, 1)
                need(dve, a_sd, i + 1)
                invert(at, 1, C2)
                at.link(scaled(Xc, Xc, 1, C2))
                dve.tensor_tensor(T1[:, cols, :], Xc, over_f(dinv[:, cols], C2), ALU.mult).then_inc(v_y1, 1)
                assert at.n == K_A2, at.n
            base += K_A2 * LOOPS

            def weigh(at, i, s, stage):
                c = i * 2 + s
                dve.wait_ge(s_gy[s], (i + (1 + stage * LOOPS)) * (16 * C))
                dve.tensor_tensor(sc_in[:, :, 1:C + 1], y_ring[:, s, :, :].rearrange("p t f -> p f t"),
                                  w_eff[:, bass.ds(c * C, C)].rearrange("p (o t) -> p o t", o=1)
                                  .broadcast_to([P, D, C]), ALU.mult).then_inc(v_y, 1)
                scan(at, c)

            def dense_x1(at, k, pn=P, rn=R):
                dve.wait_ge(s_xin, (k + 1) * 16)
                norm_sum(at, xin[0:pn, 0:rn, :], 3, rn, pn)
                centre(x1d[0:pn, 0:rn, :], xin[0:pn, 0:rn, :], 3, rn, pn).then_inc(v_dxc, 1)
                need(dve, a_dsq, k + 1)
                norm_squares(sqd[0:pn, 0:rn, :], 4, rn, pn).then_inc(v_dss, 1)
                need(dve, a_dsd, k + 1)
                invert(at, 4, rn, pn)
                scaled(x1d[0:pn, 0:rn, :], x1d[0:pn, 0:rn, :], 4, rn, pn).then_inc(v_dx1, 1)
                need(dve, v_dx1, k + 1)

            def dense_out(at, k, w0, pn=P, rn=R, banks=BANKS):
                for b, n in enumerate(banks):
                    need(dve, t_dh, w0 + b + 1)
                    r = 4 * sum(banks[0:b])
                    rows = x1d[0:pn, r:r + 4 * n, :]
                    dve.scalar_tensor_tensor(
                        out=rd[0:pn, r:r + 4 * n, :].rearrange("p a b -> p (a b)"),
                        in0=hd_ps[b % 2][0:pn, 0:n * P], scalar=0.0,
                        in1=rows.rearrange("p a b -> p (a b)"), op0=ALU.max, op1=ALU.add).then_inc(v_dh, 1)
                need(dve, v_dh, w0 + len(banks))
                norm_sum(at, rd[0:pn, 0:rn, :], 3, rn, pn)
                centre(rd[0:pn, 0:rn, :], rd[0:pn, 0:rn, :], 3, rn, pn).then_inc(v_dxc2, 1)
                need(dve, a_dsq2, k + 1)
                norm_squares(sqd[0:pn, 0:rn, :], 4, rn, pn).then_inc(v_dss2, 1)
                need(dve, a_dsd2, k + 1)
                invert(at, 4, rn, pn)
                need(dve, o_od, k)
                scaled(od[0:pn, 0:rn, :], rd[0:pn, 0:rn, :], 4, rn, pn).then_inc(v_od, 1)

            K_B = 10

            def both(at, i, k, stage):
                weigh(at, i, 0, stage)
                dense_x1(at, k)
                weigh(at, i, 1, stage)
                dense_out(at, k, k * 4)

            with dve.Fori(0, LOOPS) as i:
                at = Steps(i * K_B + base)
                both(at, i, i, 0)
                assert at.n == K_B, at.n
            base += K_B * LOOPS
            at = Steps(base)
            carry(2, at)
            base += at.n

            K_B2 = 2
            with dve.Fori(0, LOOPS) as i:
                at = Steps(i * K_B2 + base)
                cols = bass.ds(i * C2, C2)
                Sc = S[:, bass.ds(i * C2 + 1, C2), :]
                at.link(dve.tensor_tensor(corr[:, :, :], over_f(pre[:, cols], C2), over_t(car[:, :], C2), ALU.mult))
                at.link(dve.tensor_tensor(T1[:, cols, :], Sc, corr[:, :, :], ALU.add))
                dve.tensor_tensor(Sc, T1[:, cols, :], over_f(ndinv2[:, cols], C2), ALU.mult).then_inc(v_y2, 1)
                assert at.n == K_B2, at.n
            base += K_B2 * LOOPS

            dve.wait_ge(s_y2, 16 * LOOPS)
            with dve.Fori(0, NK - LOOPS) as i:
                at = Steps(i * K_B + base)
                both(at, i, i + LOOPS, 1)
            base += K_B * (NK - LOOPS)
            at = Steps(base)
            weigh(at, NK - LOOPS, 0, 1)
            dense_x1(at, NK, TAILP, TAILR)
            weigh(at, NK - LOOPS, 1, 1)
            dense_out(at, NK, NK * 4, TAILP, TAILR, [1])
            carry(3, at)
            base += at.n

            K_F = 8
            with dve.Fori(0, LOOPS) as i:
                at = Steps(i * K_F + base)
                for s in range(2):
                    c = i * 2 + s
                    cols = bass.ds(c * C, C)
                    cr = corr[:, 0:C, :]
                    need(dve, v_o, c)
                    at.link(dve.tensor_tensor(cr, over_f(pre[:, cols], C), over_t(car[:, :], C), ALU.mult))
                    at.link(dve.tensor_tensor(cr, S[:, bass.ds(c * C + 1, C), :], cr, ALU.add))
                    need(dve, t_ZT, c * 4)
                    dve.tensor_tensor(Z[:, :, D:2 * D], T1[:, cols, :], over_f(ndinv[:, cols], C), ALU.mult)
                    dve.tensor_tensor(Z[:, :, 2 * D:3 * D], cr, over_f(n2dinv[:, cols], C), ALU.mult).then_inc(v_z, 1)
                    need(dve, t_hf, c * 4 + 4)
                    dve.scalar_tensor_tensor(out=cr, in0=hf_ps[:, 0:C * D].rearrange("p (t f) -> p t f", f=D),
                                             scalar=0.0, in1=X1[:, cols, :], op0=ALU.max,
                                             op1=ALU.add).then_inc(v_fh, 1)
                    need(dve, v_fh, c + 1)
                    norm_sum(at, cr, 6, C)
                    centre(cr, cr, 6, C).then_inc(v_fxc, 1)
                    need(dve, a_fsq, c + 1)
                    norm_squares(sqf[:, 0:C, :], 7, C).then_inc(v_fss, 1)
                    need(dve, a_fsd, c + 1)
                    invert(at, 7, C)
                    need(dve, o_sc, c - 1)
                    scaled(o_ring[:, s, :, :], cr, 7, C).then_inc(v_o, 1)
                assert at.n == K_F, at.n


_INS = ["x", "src", "dst", "edge_weight", "L0_gnn_W1", "L0_gnn_b1", "L0_gnn_W2", "L0_gnn_b2",
        "L0_gnn_W3", "L0_gnn_b3", "L0_gnn_W4", "L0_gnn_b4", "L1_gnn_W", "L1_gnn_b"]


def kernel(**inputs):
    import numpy as _np
    import concourse.bacc as _bacc
    from concourse import mybir as _mybir
    from concourse.bass_utils import run_bass_kernel_spmd as _run

    nc = _bacc.Bacc("TRN2", target_bir_lowering=False, num_devices=1)
    arrays, args = {}, []
    for name in _INS:
        a = _np.ascontiguousarray(inputs[name])
        arrays[f"in_{name}_dram"] = a
        args.append(nc.dram_tensor(f"in_{name}_dram", a.shape, _mybir.dt.from_np(a.dtype), kind="ExternalInput").ap())
    shape = inputs["x"].shape
    o = nc.dram_tensor("out_0_dram", shape, _mybir.dt.float32, kind="ExternalOutput").ap()
    build(nc, *args, o)
    r = _run(nc, [arrays], core_ids=[0])
    return r.results[0]["out_0_dram"]
```

```python
from contextlib import ExitStack

import concourse.bass as bass
from concourse import mybir

ALU = mybir.AluOpType
ACT = mybir.ActivationFunctionType
AX = mybir.AxisListType.X
F32 = mybir.dt.float32
I32 = mybir.dt.int32
F16 = mybir.dt.float16
BF16 = mybir.dt.bfloat16

P = 128
BIG = 1 << 20
PAD = (1 << 17) - 4
EPS = 1e-5
OFF = 2


def build(nc, x, src, dst, edge_weight, W1, b1, W2, b2, W3, b3, W4, b4, Wc, bc, out):
    N, D = x.shape
    E = src.shape[0]
    H1, H2, H3 = W1.shape[1], W2.shape[1], W3.shape[1]
    C = 14
    T = -(-E // (P * 2 * C)) * 2 * C
    LOOPS = T // (2 * C)
    FULL, REM = E // T, E % T
    PAIRS = [4, 3]
    UNITS = C // 2
    C2 = 2 * C
    R = 60
    NK = 13
    TAILP, TAILR = 40, 4
    assert P * R * NK + TAILP * TAILR == N and 2 * D == H1 and sum(PAIRS) == UNITS
    BANKS = [4, 4, 4, 3]
    FBANKS = [4, 4, 4, 2]
    BROWS = 96
    RT32 = float(D) ** 0.5
    B_BOTH = LOOPS - 1
    C_BOTH = NK - B_BOTH - 1

    ctx = ExitStack()
    with ctx:
        def sb(name, shape, dt=F32):
            return ctx.enter_context(nc.sbuf_tensor(name, shape, dt))

        def sem(name):
            return ctx.enter_context(nc.semaphore(name))

        dst_x = sb("dst_x", [P, T + 2], I32)
        dst_up = sb("dst_up", [P, T], I32)
        src_i = sb("src_i", [P, T], I32)
        w = sb("w", [P, T])
        dst1 = sb("dst1", [P, T + 2])
        src4 = sb("src4", [P, T + 4])
        d_first = sb("d_first", [P, P])
        d_diff = sb("d_diff", [P, T])
        d_delta = sb("d_delta", [P, 2, T], F16)
        cont = sb("cont", [P, T])
        last = sb("last", [P, T])
        pre = sb("pre", [P, T])
        cnt = sb("cnt", [P, T])
        rcnt = sb("rcnt", [P, T])
        prer = sb("prer", [P, T])
        deg = sb("deg", [P, T])
        dinv = sb("dinv", [P, T])
        ndinv = sb("ndinv", [P, T])
        ndinv2 = sb("ndinv2", [P, T])
        n2dinv = sb("n2dinv", [P, T])
        above = sb("above", [P, T + 4])
        below = sb("below", [P, T])
        same = sb("same", [P, T])
        w_eff = sb("w_eff", [P, T])
        tmp = sb("tmp", [P, T])
        hits = sb("hits", [P, 4, T])
        ones = sb("ones", [P, T])
        epsc = sb("epsc", [P, 1])
        zeros = sb("zeros", [P, T])
        slot_i = sb("slot_i", [P, T], I32)
        scat_i = sb("scat_i", [P, T], I32)
        X1 = sb("X1", [P, T, D])
        S = sb("S", [P, T, D])
        T1 = sb("T1", [P, T, D])
        x_ring = sb("x_ring", [P, 2, C, 2 * D])
        y_ring = sb("y_ring", [P, 2, C, D])
        o_ring = sb("o_ring", [P, 2, C, D])
        di_ring = sb("di_ring", [P, 2, C], I32)
        si_ring = sb("si_ring", [P, 2, C], I32)
        mk = sb("mk", [P, D, C + 1])
        sc_in = sb("sc_in", [P, D, C + 1])
        sc_out = sb("sc_out", [P, D, C + 1])
        corr = sb("corr", [P, C2, D])
        cz = sb("cz", [P, C, D])
        diag = sb("diag", [P, P])
        xT = sb("xT", [P, 512])
        h1 = sb("h1", [P, 512])
        h2 = sb("h2", [P, 2, 512])
        h3 = sb("h3", [P, 512])
        le = sb("le", [P, 2, 2, P], F16)
        leT = sb("leT", [P, 2, 2 * P], F16)
        w1s = sb("w1s", [P, P])
        w1b = sb("w1b", [P, P])
        w2s = sb("w2s", [P, 2, H2])
        w3s = sb("w3s", [P, 2, P])
        w4s = sb("w4s", [P, 2 * D])
        b1c = sb("b1c", [P, 1])
        b2c = sb("b2c", [P, 1])
        b3c = sb("b3c", [P, 1])
        b4r = sb("b4r", [P, D])
        ident = sb("ident", [P, P])
        ident16 = sb("ident16", [P, P], F16)
        wd = sb("wd", [P, P])
        wd2 = sb("wd2", [P, P])
        wf = sb("wf", [P, D])
        wf2 = sb("wf2", [D, D])
        brow = sb("brow", [BROWS, 512])
        b_near = sb("b_near", [BROWS, 512], BF16)
        b_parts = sb("b_parts", [BROWS, 512], BF16)
        onerow = sb("onerow", [BROWS, P], BF16)
        tails = sb("tails", [P, D])
        spans = sb("spans", [P, D])
        rstd = sb("rstd", [P, T])
        tailT = sb("tailT", [D, P])
        spanT = sb("spanT", [D, P])
        carT = sb("carT", [D, P])
        car = sb("car", [P, 4, D])
        carc = sb("carc", [P, D])
        xin = sb("xin", [P, R, D])
        x1d = sb("x1d", [P, R, D])
        sqd = sb("sqd", [P, R, D])
        rd = sb("rd", [P, R, D])
        od = sb("od", [P, R, D])
        x1T = sb("x1T", [P, 2, 512])
        st = sb("st", [P, 8, R])
        Z = [a[:, :, :].rearrange("p r f -> p (r f)")[:, 0:C * 4 * D].rearrange("p (t f) -> p t f", f=4 * D)
             for a in (xin, x1d)]
        ZT = sb("ZT", [P, 2, 512])
        sqf = sb("sqf", [P, C2, D])

        bank = [ctx.enter_context(nc.psum_tensor(f"bank{i}", [P, 512], F32)) for i in range(8)]
        leT16_ps = bank[6][:, :].bitcast(F16)
        xT_ps, h1_ps, h3_ps, m_ps, dq_ps = (bank[i] for i in (0, 1, 4, 5, 7))
        h2_ps = [bank[2], bank[3]]
        car_ps = bank[6]
        x1T_ps = [bank[0], bank[1]]
        hd_ps = [bank[2], bank[3]]
        ZT_ps = [bank[4], bank[5]]
        hf_ps = bank[7]

        y1_dram = nc.dram_tensor("y1_by_slot", [P * T, D], F32, kind="Internal").ap()
        y2_dram = nc.dram_tensor("y2_by_slot", [P * T, D], F32, kind="Internal").ap()

        s_nodes = sem("s_nodes")
        s_edges = sem("s_edges")
        s_wts = sem("s_wts")
        s_gx = [sem(f"s_gx{i}") for i in range(2)]
        s_gy = [sem(f"s_gy{i}") for i in range(2)]
        s_sc = [sem(f"s_sc{i}") for i in range(2)]
        s_y1 = sem("s_y1")
        s_y2 = sem("s_y2")
        s_xin = sem("s_xin")
        s_od = sem("s_od")
        o_od = sem("o_od")
        o_sc = sem("o_sc")
        p_id = sem("p_id")
        p_idx = sem("p_idx")
        p_begun = sem("p_begun")
        v_fill = sem("v_fill")
        v_rings = sem("v_rings")
        v_scan = sem("v_scan")
        v_carc = sem("v_carc")
        v_x1 = sem("v_x1")
        v_const = sem("v_const")
        p_corr = sem("p_corr")
        a_mk = sem("a_mk")
        a_S = sem("a_S")
        v_deg = sem("v_deg")
        v_ss = sem("v_ss")
        v_dss = sem("v_dss")
        v_dss2 = sem("v_dss2")
        v_fss = sem("v_fss")
        v_pad = sem("v_pad")
        v_wts = sem("v_wts")
        v_diag = sem("v_diag")
        v_tail = sem("v_tail")
        v_ct = sem("v_ct")
        v_le = sem("v_le")
        v_cnt = sem("v_cnt")
        v_m = sem("v_m")
        v_slot = sem("v_slot")
        v_y = sem("v_y")
        v_xc = sem("v_xc")
        v_y1 = sem("v_y1")
        v_y2 = sem("v_y2")
        v_scat = sem("v_scat")
        v_dxc = sem("v_dxc")
        v_dx1 = sem("v_dx1")
        v_dh = sem("v_dh")
        v_dxc2 = sem("v_dxc2")
        v_od = sem("v_od")
        v_z = sem("v_z")
        v_fh = sem("v_fh")
        v_fxc = sem("v_fxc")
        v_o = sem("v_o")
        v_step = sem("v_step")
        t_d0 = sem("t_d0")
        t_tail = sem("t_tail")
        t_ct = sem("t_ct")
        t_leT = sem("t_leT")
        t_dq = sem("t_dq")
        t_xT = sem("t_xT")
        t_h1 = sem("t_h1")
        t_h2 = sem("t_h2")
        t_h3 = sem("t_h3")
        t_m = sem("t_m")
        t_dT = sem("t_dT")
        t_dh = sem("t_dh")
        t_ZT = sem("t_ZT")
        t_hf = sem("t_hf")
        a_deg = sem("a_deg")
        a_sd = sem("a_sd")
        a_dsd = sem("a_dsd")
        a_dsd2 = sem("a_dsd2")
        a_fsd = sem("a_fsd")
        a_leT = sem("a_leT")
        a_xT = sem("a_xT")
        a_h1 = sem("a_h1")
        a_h2 = sem("a_h2")
        a_h3 = sem("a_h3")
        a_xd = sem("a_xd")
        a_sq = sem("a_sq")
        a_dsq = sem("a_dsq")
        a_dT = sem("a_dT")
        a_dsq2 = sem("a_dsq2")
        a_z = sem("a_z")
        a_ZT = sem("a_ZT")
        a_fsq = sem("a_fsq")

        def need(eng, s, n):
            eng.wait_ge(s, n + OFF)

        def over_f(a, n):
            return a.rearrange("p (n o) -> p n o", o=1).broadcast_to([a.shape[0], n, D])

        def over_t(a, n):
            return a.rearrange("p (o f) -> p o f", o=1).broadcast_to([a.shape[0], n, D])

        y1_st = y1_dram.rearrange("(p t) f -> p t f", p=P)
        y2_st = y2_dram.rearrange("(p t) f -> p t f", p=P)
        x_d = x[0:P * R * NK, :].rearrange("(p r) f -> p r f", p=P)
        out_d = out[0:P * R * NK, :].rearrange("(p r) f -> p r f", p=P)
        x_tail = x[P * R * NK:N, :].rearrange("(p r) f -> p r f", r=TAILR)
        out_tail = out[P * R * NK:N, :].rearrange("(p r) f -> p r f", r=TAILR)

        NODE_DMAS, EDGE_DMAS = 4, 5
        WT_DMAS = 32
        block = ctx.enter_context(nc.Block())

        @block.sync
        def _(sp):
            def edge_rows(a, s0, p0, n, m):
                return a[s0:s0 + n * T].rearrange("(p t) -> p t", t=T)[:, 0:m] if n > 1 else \
                    a[s0:s0 + m].rearrange("(p t) -> p t", p=1)

            sp.sem_inc(o_od, OFF)
            sp.sem_inc(o_sc, OFF)
            sp.wait_ge(v_pad, 4)
            sp.dma_start(dst_x[0:FULL, 1:T + 1], edge_rows(dst, 0, 0, FULL, T)).then_inc(s_nodes, 16)
            sp.dma_start(dst_x[FULL:P, 1:REM + 1], edge_rows(dst, FULL * T, 0, 1, REM)).then_inc(s_nodes, 16)
            sp.dma_start(src_i[0:FULL, :], edge_rows(src, 0, 0, FULL, T)).then_inc(s_nodes, 16)
            sp.dma_start(src_i[FULL:P, 0:REM], edge_rows(src, FULL * T, 0, 1, REM)).then_inc(s_nodes, 16)
            sp.dma_start(w[0:FULL, :], edge_rows(edge_weight, 0, 0, FULL, T)).then_inc(s_edges, 16)
            sp.dma_start(w[FULL:P, 0:REM], edge_rows(edge_weight, FULL * T, 0, 1, REM)).then_inc(s_edges, 16)
            sp.dma_start(dst_up[1:P, :], edge_rows(dst, 0, 0, FULL, T)).then_inc(s_edges, 16)
            with nc.allow_non_contiguous_dma(reason="one neighbour for each partition"):
                sp.dma_start(dst_x[1:P, 0:1], edge_rows(dst, 0, 0, FULL, T)[:, T - 1:T]).then_inc(s_edges, 16)
                sp.dma_start(dst_x[0:FULL - 1, T + 1:T + 2],
                             edge_rows(dst, T, 0, FULL - 1, T)[:, 0:1]).then_inc(s_edges, 16)

            sp.wait_ge(v_fill, 8)

            def wt(o, i):
                sp.dma_start(o, i).then_inc(s_wts, 16)

            for g in range(2):
                h = g * H1
                wt(w1s[h:h + D, h:h + H1], W1[0:D, :])
                wt(w1s[h + D:h + 2 * D, h:h + H1], W1[D:2 * D, :])
                wt(w1b[h:h + D, h:h + H1], W1[D:2 * D, :])
                wt(w2s[h:h + H1, g, :], W2[:, :])
                wt(w3s[:, g, h:h + H3], W3[:, :])
                wt(w4s[h:h + H3, g * D:(g + 1) * D], W4[:, :])
                wt(b1c[h:h + H1, :], b1.rearrange("(p o) -> p o", o=1))
                wt(b3c[h:h + H3, :], b3.rearrange("(p o) -> p o", o=1))
            wt(b2c[:, :], b2.rearrange("(p o) -> p o", o=1))
            wt(b4r[:, :], b4.rearrange("(o f) -> o f", o=1).broadcast_to([P, D]))
            for g in range(4):
                h = g * D
                wt(wd[h:h + D, h:h + D], Wc[0])
                wt(wd2[h:h + D, h:h + D], Wc[2])
            wt(wf[0:D, :], Wc[0])
            wt(wf2[:, :], Wc[2])
            wt(wf[D:2 * D, :], Wc[1])
            wt(wf[2 * D:3 * D, :], Wc[2])
            wt(wf[3 * D:3 * D + 1, :], bc.rearrange("(o f) -> o f", o=1))
            wt(brow.rearrange("o (r f) -> o r f", f=D),
               bc.rearrange("(o r f) -> o r f", o=1, r=1).broadcast_to([BROWS, 512 // D, D]))

            sp.dma_start(xin[:, :, :], x_d[:, 0:R, :]).then_inc(s_xin, 16)
            with sp.Fori(0, LOOPS) as i:
                need(sp, v_y1, i + 1)
                sp.dma_start(y1_st[:, bass.ds(i * C2, C2), :], T1[:, bass.ds(i * C2, C2), :]).then_inc(s_y1, 16)

            def load(k):
                need(sp, v_dxc, k)
                sp.dma_start(xin[:, :, :], x_d[:, bass.ds(k * R, R), :]).then_inc(s_xin, 16)

            def store(k):
                need(sp, v_od, k + 1)
                sp.dma_start(out_d[:, bass.ds(k * R, R), :], od[:, :, :]).then_inc(s_od, 16)
                sp.wait_ge(s_od, (k + 1) * 16)
                sp.sem_inc(o_od)

            load(1)
            with sp.Fori(1, LOOPS) as k:
                load(k + 1)
                store(k - 1)
            with sp.Fori(0, LOOPS) as i:
                need(sp, v_y2, i + 1)
                sp.dma_start(y2_st[:, bass.ds(i * C2, C2), :], T1[:, bass.ds(i * C2, C2), :]).then_inc(s_y2, 16)
            with sp.Fori(LOOPS, NK - 1) as k:
                load(k + 1)
                store(k - 1)
            need(sp, v_dxc, NK)
            sp.dma_start(xin[0:TAILP, 0:TAILR, :], x_tail).then_inc(s_xin, 16)
            store(NK - 2)
            store(NK - 1)
            need(sp, v_od, NK + 1)
            sp.dma_start(out_tail, od[0:TAILP, 0:TAILR, :]).then_inc(s_od, 16)
            sp.wait_ge(s_od, 16 * (NK + 1))

            with sp.Fori(0, LOOPS) as i:
                for s in range(2):
                    sp.wait_ge(s_sc[s], (i + 1) * (16 * C))
                    sp.sem_inc(o_sc)

        @block.gpsimd
        def _(pool):
            pool.sem_inc(p_idx, OFF)
            pool.sem_inc(p_corr, OFF)
            top_node = pool.to_reg(N - 1)
            top_slot = pool.to_reg(P * T - 1)
            nc.gpsimd.memset(ident[:, :], 0.0).then_inc(p_id, 1)
            pool.wait_ge(p_id, 1)
            nc.gpsimd.affine_select(out=ident[:, :], in_=ident[:, :], compare_op=ALU.not_equal, fill=1.0,
                                    base=0, pattern=[[-1, P]], channel_multiplier=1).then_inc(p_id, 1)

            def rows(s, ring, table, idx, k, top, done):
                nc.gpsimd.indirect_dma_start(
                    out=ring, out_offset=None, in_=table,
                    in_offset=bass.IndirectOffsetOnAxis(ap=idx[:, s, k:k + 1], axis=0),
                    bounds_check=top, oob_is_err=False).then_inc(done, 16)

            pool.wait_ge(s_nodes, 16 * NODE_DMAS)
            pool.wait_ge(v_rings, 2)
            with pool.Fori(0, LOOPS) as i:
                for s in range(2):
                    c = i * 2 + s
                    need(pool, a_xd, c - 1)
                    nc.gpsimd.tensor_copy(di_ring[:, s, :], dst_x[:, bass.ds(c * C + 1, C)]).then_inc(p_idx, 1)
                    nc.gpsimd.tensor_copy(si_ring[:, s, :], src_i[:, bass.ds(c * C, C)]).then_inc(p_idx, 1)
                    need(pool, p_idx, c * 2 + 2)
                    pool.sem_inc(p_begun)
                    for k in range(C):
                        rows(s, x_ring[:, s, k, 0:D], x[:, :], di_ring, k, top_node, s_gx[s])
                        rows(s, x_ring[:, s, k, D:2 * D], x[:, :], si_ring, k, top_node, s_gx[s])

            pool.wait_ge(v_carc, 1)
            with pool.Fori(0, LOOPS) as i:
                cols = bass.ds(i * C2, C2)
                nc.gpsimd.tensor_tensor(T1[:, cols, :], over_f(prer[:, cols], C2), over_t(carc[:, :], C2),
                                        ALU.mult).then_inc(p_corr, 1)

            pool.wait_ge(v_slot, 1)
            for stage, (stored, table) in enumerate(((s_y1, y1_dram), (s_y2, y2_dram))):
                pool.wait_ge(stored, 16 * LOOPS)
                with pool.Fori(0, LOOPS) as i:
                    for s in range(2):
                        c = i * 2 + s + stage * 2 * LOOPS
                        need(pool, v_y, c - 1)
                        nc.gpsimd.tensor_copy(si_ring[:, s, :], slot_i[:, bass.ds((i * 2 + s) * C, C)]).then_inc(p_idx, 1)
                        need(pool, p_idx, c + 4 * LOOPS + 1)
                        pool.sem_inc(p_begun)
                        for k in range(C):
                            rows(s, y_ring[:, s, k, :], table[:, :], si_ring, k, top_slot, s_gy[s])

            pool.wait_ge(s_od, 16 * (NK + 1))
            with pool.Fori(0, LOOPS) as i:
                for s in range(2):
                    c = i * 2 + s
                    need(pool, o_sc, c - 1)
                    nc.gpsimd.tensor_copy(di_ring[:, s, :], scat_i[:, bass.ds(c * C, C)]).then_inc(p_idx, 1)
                    need(pool, p_idx, c + 8 * LOOPS + 1)
                    need(pool, v_o, c + 1)
                    pool.sem_inc(p_begun)
                    for k in range(C):
                        nc.gpsimd.indirect_dma_start(
                            out=out[:, :], out_offset=bass.IndirectOffsetOnAxis(ap=di_ring[:, s, k:k + 1], axis=0),
                            in_=o_ring[:, s, k, :], in_offset=None,
                            bounds_check=top_node, oob_is_err=False).then_inc(s_sc[s], 16)
            for s in range(2):
                pool.wait_ge(s_sc[s], 16 * C * LOOPS)

        @block.tensor
        def _(pe):
            for q in (t_leT, t_dq, t_xT, t_h1, t_h2, t_h3, t_m, t_dT, t_dh, t_ZT, t_hf):
                pe.sem_inc(q, OFF)
            pe.wait_ge(p_id, 2)

            def carry(k):
                pe.wait_ge(v_tail, k + 1)
                ins = pe.transpose(car_ps[0:D, 0:P], tails[:, :], ident[:, :])
                if k == 0:
                    ins = pe.transpose(car_ps[0:D, P:2 * P], spans[:, :], ident[:, :])
                ins.then_inc(t_tail, 1)
                pe.wait_ge(v_ct, k + 1)
                pe.transpose(car_ps[:, 2 * P:2 * P + D], carT[:, :], ident[0:D, 0:D]).then_inc(t_ct, 1)

            pe.wait_ge(v_diag, 1)
            pe.matmul(dq_ps[:, 0:P], ones[:, 0:P], diag[:, :], start=True, stop=True).then_inc(t_d0, 1)
            carry(0)
            pe.wait_ge(v_wts, 1)

            def look_T(c, u, s):
                U, b = c * UNITS + u, (s + u) % 2
                need(pe, v_le, U + 1)
                need(pe, a_leT, U)
                for j in range(2):
                    ins = pe.transpose(leT16_ps[:, j * P:(j + 1) * P], le[:, b, j, :], ident16[:, :])
                ins.then_inc(t_leT, 1)

            def look_D(c, u, s):
                U, b = c * UNITS + u, (s + u) % 2
                need(pe, a_leT, U + 1)
                need(pe, v_cnt, U)
                for j in range(2):
                    for part in range(2):
                        ins = pe.matmul(dq_ps[:, j * T:(j + 1) * T], leT[:, b, j * P:(j + 1) * P],
                                        d_delta[:, part, :], start=(part == 0), stop=(part == 1))
                ins.then_inc(t_dq, 1)

            def mlp_T(i, c, v, s):
                if v == 0:
                    pe.wait_ge(s_gx[s], (i + 1) * (32 * C))
                need(pe, a_xT, c * 2 + v)
                for q in range(PAIRS[v]):
                    t = 2 * (q + v * PAIRS[0])
                    ins = pe.transpose(xT_ps[:, q * P:(q + 1) * P],
                                       x_ring[:, s, t:t + 2, :].rearrange("p a b -> p (a b)"), ident[:, :])
                ins.then_inc(t_xT, 1)

            def mlp_1(c, v):
                n = PAIRS[v] * P
                need(pe, a_xT, c * 2 + v + 1)
                need(pe, a_h1, c * 2 + v)
                pe.matmul(h1_ps[:, 0:n], w1s[:, :], xT[:, 0:n], start=True, stop=True).then_inc(t_h1, 1)

            def mlp_2(c, v):
                n = PAIRS[v] * P
                need(pe, a_h1, c * 2 + v + 1)
                for g in range(2):
                    need(pe, a_h2, c * 4 + 2 * v + g - 1)
                    pe.matmul(h2_ps[g][:, 0:n], w2s[:, g, :], h1[:, 0:n], start=True, stop=True).then_inc(t_h2, 1)

            def mlp_3(c, v):
                n = PAIRS[v] * P
                need(pe, a_h2, c * 4 + 2 * v + 2)
                need(pe, a_h3, c * 2 + v)
                for g in range(2):
                    ins = pe.matmul(h3_ps[:, 0:n], w3s[:, g, :], h2[:, g, 0:n], start=(g == 0), stop=(g == 1))
                ins.then_inc(t_h3, 1)

            def mlp_4(c, v):
                need(pe, a_h3, c * 2 + v + 1)
                if v == 0:
                    need(pe, v_m, c)
                for q in range(PAIRS[v]):
                    g = q + v * PAIRS[0]
                    ins = pe.matmul(m_ps[:, g * 2 * D:(g + 1) * 2 * D], h3[:, q * P:(q + 1) * P], w4s[:, :],
                                    start=True, stop=True)
                ins.then_inc(t_m, 1)

            with pe.Fori(0, LOOPS) as i:
                for s in range(2):
                    c = i * 2 + s
                    def look(j):
                        if j < UNITS:
                            look_T(c, j, s)
                        if j > 0:
                            look_D(c, j - 1, s)

                    look(0)
                    mlp_T(i, c, 0, s)
                    look(1)
                    mlp_1(c, 0)
                    look(2)
                    mlp_2(c, 0)
                    mlp_T(i, c, 1, s)
                    look(3)
                    mlp_3(c, 0)
                    mlp_1(c, 1)
                    look(4)
                    mlp_4(c, 0)
                    mlp_2(c, 1)
                    look(5)
                    mlp_3(c, 1)
                    look(6)
                    look(7)
                    mlp_4(c, 1)
            carry(1)

            def dense(k, banks, pn, w0):
                def turn(b):
                    need(pe, a_dT, w0 + b - 1)
                    for g in range(banks[b]):
                        r = 4 * (g + sum(banks[0:b]))
                        ins = pe.transpose(x1T_ps[b % 2][:, g * P:g * P + pn],
                                           x1d[0:pn, r:r + 4, :].rearrange("p a b -> p (a b)"),
                                           ident[0:pn, 0:pn])
                    ins.then_inc(t_dT, 1)

                need(pe, v_dx1, k + 1)
                turn(0)
                for b in range(len(banks)):
                    if b + 1 < len(banks):
                        turn(b + 1)
                    n = banks[b]
                    need(pe, a_dT, w0 + b + 1)
                    need(pe, v_dh, w0 + b - 1)
                    pe.matmul(hd_ps[b % 2][0:pn, 0:n * P], onerow[:, 0:pn], b_parts[:, 0:n * P], start=True, stop=False,
                              skip_group_check=True)
                    for g in range(n):
                        ins = pe.matmul(hd_ps[b % 2][0:pn, g * P:(g + 1) * P], x1T[:, b % 2, g * P:g * P + pn],
                                        wd[:, :], start=False, stop=(g == n - 1), skip_group_check=True)
                    ins.then_inc(t_dh, 1)

            with pe.Fori(0, B_BOTH) as k:
                dense(k, BANKS, P, k * 4)
            carry(2)
            with pe.Fori(B_BOTH, NK) as k:
                dense(k, BANKS, P, k * 4)
            dense(NK, [1], TAILP, NK * 4)
            carry(3)

            with pe.Fori(0, LOOPS) as i:
                for s in range(2):
                    c = i * 2 + s
                    need(pe, v_z, c + 1)
                    need(pe, a_z, c + 1)
                    need(pe, v_fh, c)

                    def turn(b):
                        need(pe, a_ZT, c * 4 + b - 1)
                        for g in range(FBANKS[b]):
                            ins = pe.transpose(ZT_ps[b % 2][:, g * P:(g + 1) * P], Z[s][:, g + 4 * b, :], ident[:, :])
                        ins.then_inc(t_ZT, 1)

                    turn(0)
                    for b in range(4):
                        if b < 3:
                            turn(b + 1)
                        need(pe, a_ZT, c * 4 + b + 1)
                        for g in range(FBANKS[b]):
                            t = g + 4 * b
                            ins = pe.matmul(hf_ps[:, t * D:(t + 1) * D], ZT[:, b % 2, g * P:(g + 1) * P], wf[:, :],
                                            start=True, stop=True)
                        ins.then_inc(t_hf, 1)

        @block.scalar
        def _(act):
            for q in (a_leT, a_xT, a_h1, a_h2, a_h3, a_xd, a_sq, a_dsq, a_dT, a_dsq2, a_z, a_ZT, a_fsq,
                      a_sd, a_dsd, a_dsd2, a_fsd, a_mk, a_S):
                act.sem_inc(q, OFF)
            act.wait_ge(v_deg, 1)
            nc.scalar.activation(dinv[:, :], dinv[:, :], ACT.Sqrt).then_inc(a_deg, 1)
            act.wait_ge(s_wts, 16 * WT_DMAS)
            act.wait_ge(v_fill, 9)

            def deviation(ss, n, pn=P):
                return nc.scalar.activation(st[0:pn, ss, 0:n], st[0:pn, ss, 0:n], ACT.Sqrt, bias=epsc[0:pn, 0:1])

            def look(c, u, s):
                U, b = c * UNITS + u, (s + u) % 2
                need(act, t_leT, U + 1)
                need(act, t_dq, U - 1)
                nc.scalar.copy(leT[:, b, :], leT16_ps[:, 0:2 * P]).then_inc(a_leT, 1)

            def x_T(c, v):
                n = PAIRS[v] * P
                need(act, t_xT, c * 2 + v + 1)
                need(act, t_h1, c * 2 + v)
                nc.scalar.copy(xT[:, 0:n], xT_ps[:, 0:n]).then_inc(a_xT, 1)

            def relu_1(c, v):
                n = PAIRS[v] * P
                need(act, t_h1, c * 2 + v + 1)
                need(act, t_h2, c * 4 + 2 * v)
                nc.scalar.activation(h1[:, 0:n], h1_ps[:, 0:n], ACT.Relu, bias=b1c[:, 0:1]).then_inc(a_h1, 1)

            def relu_2(c, v):
                n = PAIRS[v] * P
                need(act, t_h3, c * 2 + v)
                for g in range(2):
                    need(act, t_h2, c * 4 + 2 * v + g + 1)
                    nc.scalar.activation(h2[:, g, 0:n], h2_ps[g][:, 0:n], ACT.Relu, bias=b2c[:, 0:1]).then_inc(a_h2, 1)

            def relu_3(c, v):
                n = PAIRS[v] * P
                need(act, t_h3, c * 2 + v + 1)
                need(act, t_m, c * 2 + v)
                nc.scalar.activation(h3[:, 0:n], h3_ps[:, 0:n], ACT.Relu, bias=b3c[:, 0:1]).then_inc(a_h3, 1)

            def spread_mask(c, stage):
                need(act, v_scan, c + stage * 2 * LOOPS)
                nc.scalar.copy(mk[:, :, 1:C + 1],
                               cont[:, bass.ds(c * C, C)].rearrange("p (o t) -> p o t", o=1)
                               .broadcast_to([P, D, C])).then_inc(a_mk, 1)

            def keep_sums(c, stage):
                need(act, v_scan, c + stage * 2 * LOOPS + 1)
                o = (S, T1)[stage - 1]
                nc.scalar.copy(o[:, bass.ds(c * C, C), :],
                               sc_out[:, :, 1:C + 1].rearrange("p f t -> p t f")).then_inc(a_S, 1)

            act.wait_ge(v_const, 1)
            with act.Fori(0, LOOPS) as i:
                for s in range(2):
                    c = i * 2 + s
                    look(c, 0, s)
                    x_T(c, 0)
                    look(c, 1, s)
                    relu_1(c, 0)
                    look(c, 2, s)
                    relu_2(c, 0)
                    x_T(c, 1)
                    nc.scalar.copy(X1[:, bass.ds(c * C, C), :], x_ring[:, s, :, 0:D]).then_inc(a_xd, 1)
                    look(c, 3, s)
                    relu_3(c, 0)
                    relu_1(c, 1)
                    look(c, 4, s)
                    spread_mask(c, 0)
                    relu_2(c, 1)
                    look(c, 5, s)
                    relu_3(c, 1)
                    look(c, 6, s)

            def square(i):
                need(act, v_xc, i + 1)
                need(act, v_ss, i)
                nc.scalar.activation(sqf[:, :, :], X1[:, bass.ds(i * C2, C2), :], ACT.Square).then_inc(a_sq, 1)

            def deviate(i):
                need(act, v_ss, i + 1)
                deviation(1, C2).then_inc(a_sd, 1)

            with act.Fori(0, LOOPS) as i:
                square(i)
                deviate(i)

            def square_1(k, pn=P, rn=R):
                need(act, v_dxc, k + 1)
                nc.scalar.activation(sqd[0:pn, 0:rn, :], x1d[0:pn, 0:rn, :], ACT.Square).then_inc(a_dsq, 1)

            def deviate_1(k, pn=P, rn=R):
                need(act, v_dss, k + 1)
                deviation(4, rn, pn).then_inc(a_dsd, 1)

            def move_x1T(w0, pn=P, banks=BANKS):
                for b, n in enumerate(banks):
                    need(act, t_dT, w0 + b + 1)
                    need(act, t_dh, w0 + b - 1)
                    m = n * P if pn == P else pn
                    nc.scalar.copy(x1T[:, b % 2, 0:m], x1T_ps[b % 2][:, 0:m]).then_inc(a_dT, 1)

            def square_2(k, pn=P, rn=R):
                need(act, v_dxc2, k + 1)
                need(act, o_od, k)
                nc.scalar.activation(od[0:pn, 0:rn, :], rd[0:pn, 0:rn, :], ACT.Square).then_inc(a_dsq2, 1)

            def deviate_2(k, pn=P, rn=R):
                need(act, v_dss2, k + 1)
                deviation(5, rn, pn).then_inc(a_dsd2, 1)

            def both(i, k, stage, after=True):
                spread_mask(i * 2, stage)
                if after:
                    square_2(k - 1)
                square_1(k)
                keep_sums(i * 2, stage)
                spread_mask(i * 2 + 1, stage)
                deviate_1(k)
                if after:
                    deviate_2(k - 1)
                move_x1T(k * 4)
                keep_sums(i * 2 + 1, stage)

            both(0, 0, 1, after=False)
            with act.Fori(1, B_BOTH) as i:
                both(i, i, 1)
            spread_mask(2 * LOOPS - 2, 1)
            square_2(B_BOTH - 1)
            square_1(B_BOTH)
            keep_sums(2 * LOOPS - 2, 1)
            spread_mask(2 * LOOPS - 1, 1)
            deviate_2(B_BOTH - 1)
            keep_sums(2 * LOOPS - 1, 1)
            deviate_1(B_BOTH)
            move_x1T(B_BOTH * 4)
            act.wait_ge(s_y2, 16 * LOOPS)
            with act.Fori(0, C_BOTH) as i:
                both(i, i + (B_BOTH + 1), 2)
            spread_mask(2 * LOOPS - 2, 2)
            square_2(NK - 1)
            square_1(NK, TAILP, TAILR)
            keep_sums(2 * LOOPS - 2, 2)
            deviate_1(NK, TAILP, TAILR)
            deviate_2(NK - 1)
            move_x1T(NK * 4, TAILP, [1])
            square_2(NK, TAILP, TAILR)
            deviate_2(NK, TAILP, TAILR)
            spread_mask(2 * LOOPS - 1, 2)
            keep_sums(2 * LOOPS - 1, 2)

            def z_part(c, s):
                nc.scalar.copy(Z[s][:, :, 0:D], X1[:, bass.ds(c * C, C), :]).then_inc(a_z, 1)

            act.wait_ge(v_const, 3)
            z_part(0, 0)

            def finish(c, s, more=True):
                for b, n in enumerate(FBANKS):
                    need(act, t_ZT, c * 4 + b + 1)
                    need(act, t_hf, c * 4 + b - 1)
                    nc.scalar.copy(ZT[:, b % 2, 0:n * P], ZT_ps[b % 2][:, 0:n * P]).then_inc(a_ZT, 1)
                if more:
                    z_part(c + 1, 1 - s)
                need(act, v_fxc, c + 1)
                nc.scalar.activation(sqf[:, 0:C, :], corr[:, 0:C, :], ACT.Square).then_inc(a_fsq, 1)
                need(act, v_fss, c + 1)
                deviation(7, C).then_inc(a_fsd, 1)

            with act.Fori(0, LOOPS - 1) as i:
                finish(i * 2, 0)
                finish(i * 2 + 1, 1)
            finish(2 * LOOPS - 2, 0)
            finish(2 * LOOPS - 1, 1, more=False)

        @block.vector
        def _(dve):
            for q in (v_le, v_cnt, v_m, v_y, v_xc, v_y1, v_y2, v_dxc, v_dx1, v_dh, v_dxc2, v_od, v_z,
                      v_fh, v_fxc, v_o, v_step, v_ss, v_dss, v_dss2, v_fss,
                      v_scan, v_x1):
                dve.sem_inc(q, OFF)

            class Steps:

                def __init__(self, base):
                    self.base, self.n = base, 0

                def done(self, ins):
                    self.n += 1
                    ins.then_inc(v_step, 1)

                def seen(self):
                    need(dve, v_step, self.base + self.n)

                def link(self, ins):
                    self.done(ins)
                    self.seen()

            at = Steps(0)
            link = at.link

            dve.memset(dst_x[:, :], PAD).then_inc(v_pad, 1)
            dve.memset(src_i[:, :], PAD).then_inc(v_pad, 1)
            dve.memset(w[:, :], 0.0).then_inc(v_pad, 1)
            dve.memset(dst_up[:, :], -1).then_inc(v_pad, 1)
            dve.memset(x_ring[:, :, :, :], 0.0).then_inc(v_rings, 1)
            dve.memset(y_ring[:, :, :, :], 0.0).then_inc(v_rings, 1)
            dve.memset(w1s[:, :], 0.0).then_inc(v_fill, 1)
            dve.memset(w1b[:, :], 0.0).then_inc(v_fill, 1)
            dve.memset(w2s[:, :, :], 0.0).then_inc(v_fill, 1)
            dve.memset(w3s[:, :, :], 0.0).then_inc(v_fill, 1)
            dve.memset(w4s[:, :], 0.0).then_inc(v_fill, 1)
            dve.memset(wd[:, :], 0.0).then_inc(v_fill, 1)
            dve.memset(wd2[:, :], 0.0).then_inc(v_fill, 1)
            dve.memset(wf[:, :], 0.0).then_inc(v_fill, 1)
            dve.memset(epsc[:, :], D * EPS).then_inc(v_fill, 1)
            dve.memset(ones[:, :], 1.0)
            dve.memset(zeros[:, :], 0.0)
            dve.memset(onerow[:, :], 1.0)
            dve.memset(src4[:, :], 0.0)
            dve.memset(sc_out[:, :, :], 0.0)
            dve.memset(mk[:, :, :], 0.0).then_inc(v_const, 1)
            dve.memset(carT[:, :], 0.0)
            dve.memset(b_parts[:, :], 0.0)
            link(dve.memset(tails[:, :], 0.0))

            dve.wait_ge(s_nodes, 16 * NODE_DMAS)
            dve.wait_ge(s_edges, 16 * EDGE_DMAS)
            dve.tensor_scalar(dst1[:, :], dst_x[:, :], 1.0, None, ALU.add)
            dve.tensor_scalar(src4[:, 0:T], src_i[:, :], 1.0, 0.25, ALU.add, ALU.mult)
            link(dve.tensor_scalar(tmp[:, :], dst_up[:, :], 1.0, None, ALU.add))
            dve.wait_ge(p_id, 2)
            dve.tensor_copy(ident16[:, :], ident[:, :])
            dve.tensor_scalar(diag[:, :], ident[:, :], dst1[:, 1:2], 0.25, ALU.mult, ALU.mult).then_inc(v_diag, 1)
            link(dve.tensor_tensor(d_diff[:, :], dst1[:, 1:T + 1], tmp[:, :], ALU.subtract))
            link(dve.tensor_scalar(d_delta[:, 0, :], d_diff[:, :], 0.25, None, ALU.mult))
            dve.scalar_tensor_tensor(out=d_delta[:, 1, :], in0=d_diff[:, :], scalar=0.25, in1=d_delta[:, 0, :],
                                     op0=ALU.mult, op1=ALU.subtract)
            dve.tensor_tensor(cont[:, :], dst1[:, 0:T], dst1[:, 1:T + 1], ALU.is_equal)
            link(dve.tensor_tensor(last[:, :], dst1[:, 1:T + 1], dst1[:, 2:T + 2], ALU.not_equal))
            link(dve.tensor_scalar(tmp[:, :], dst1[:, 1:T + 1], float(BIG - 1), None, ALU.add))
            dve.scalar_tensor_tensor(out=scat_i[:, :], in0=last[:, :], scalar=-float(BIG), in1=tmp[:, :],
                                     op0=ALU.mult, op1=ALU.add).then_inc(v_scat, 1)
            dve.tensor_tensor_scan(pre[:, :], cont[:, :], zeros[:, :], 1.0, ALU.mult, ALU.add)
            dve.tensor_tensor_scan(cnt[:, :], cont[:, :], ones[:, :], 0.0, ALU.mult, ALU.add)
            link(dve.tensor_tensor_scan(deg[:, :], cont[:, :], w[:, :], 0.0, ALU.mult, ALU.add))

            def carry(k, at):
                if k == 0:
                    dve.tensor_copy(tails[:, 0:1], cnt[:, T - 1:T])
                    dve.tensor_copy(tails[:, 1:2], deg[:, T - 1:T])
                    dve.tensor_copy(spans[:, :], pre[:, T - 1:T].broadcast_to([P, D])).then_inc(v_tail, 1)
                else:
                    dve.tensor_copy(tails[:, :], sc_out[:, :, C]).then_inc(v_tail, 1)
                dve.wait_ge(t_tail, k + 1)
                if k == 0:
                    at.done(dve.tensor_copy(spanT[:, :], car_ps[0:D, P:2 * P]))
                at.link(dve.tensor_copy(tailT[:, :], car_ps[0:D, 0:P]))
                dve.tensor_tensor_scan(carT[:, 1:P], spanT[:, 0:P - 1], tailT[:, 0:P - 1], 0.0,
                                       ALU.mult, ALU.add).then_inc(v_ct, 1)
                dve.wait_ge(t_ct, k + 1)
                at.link(dve.tensor_copy(car[:, k, :], car_ps[:, 2 * P:2 * P + D]))

            dve.wait_ge(t_d0, 1)
            link(dve.tensor_copy(d_first[:, :], dq_ps[:, 0:P]))
            carry(0, at)
            dve.scalar_tensor_tensor(out=cnt[:, :], in0=pre[:, :], scalar=car[:, 0, 0:1], in1=cnt[:, :],
                                     op0=ALU.mult, op1=ALU.add)
            link(dve.scalar_tensor_tensor(out=deg[:, :], in0=pre[:, :], scalar=car[:, 0, 1:2], in1=deg[:, :],
                                          op0=ALU.mult, op1=ALU.add))
            dve.reciprocal(rcnt[:, :], cnt[:, :])
            dve.tensor_scalar(dinv[:, :], deg[:, :], 1e-12, None, ALU.max).then_inc(v_deg, 1)
            dve.tensor_scalar(tmp[:, :], deg[:, :], 0.0, None, ALU.is_gt)
            dve.wait_ge(a_deg, 1)
            link(dve.reciprocal(dinv[:, :], dinv[:, :]))
            dve.tensor_tensor(prer[:, :], pre[:, :], rcnt[:, :], ALU.mult)
            link(dve.tensor_tensor(dinv[:, :], dinv[:, :], tmp[:, :], ALU.mult))
            dve.tensor_scalar(ndinv[:, :], dinv[:, :], -1.0, None, ALU.mult)
            dve.tensor_scalar(n2dinv[:, :], dinv[:, :], -2.0, None, ALU.mult)
            link(dve.scalar_tensor_tensor(out=ndinv2[:, :], in0=dinv[:, :], scalar=-1.0, in1=dinv[:, :],
                                          op0=ALU.mult, op1=ALU.mult))

            dve.wait_ge(s_wts, 16 * WT_DMAS)
            dve.tensor_tensor(w1s[:, :], w1s[:, :], w1b[:, :], ALU.subtract)
            dve.tensor_tensor(wd[:, :], wd[:, :], wd2[:, :], ALU.subtract)
            dve.tensor_copy(b_parts[0:1, :], brow[0:1, :])
            link(dve.tensor_copy(b_near[:, :], brow[:, :]))
            link(dve.tensor_tensor(brow[:, :], brow[:, :], b_near[:, :], ALU.subtract))
            dve.tensor_copy(b_parts[32:33, :], brow[32:33, :])
            link(dve.tensor_copy(b_near[:, :], brow[:, :]))
            link(dve.tensor_tensor(brow[:, :], brow[:, :], b_near[:, :], ALU.subtract))
            dve.tensor_copy(b_parts[64:65, :], brow[64:65, :])
            dve.tensor_tensor(wf[0:D, :], wf[0:D, :], wf2[:, :], ALU.subtract).then_inc(v_wts, 1)

            def compare(c, u, s):
                U, b = c * UNITS + u, (s + u) % 2
                need(dve, t_leT, U - 1)
                for j in range(2):
                    t = c * C + (2 * u + j)
                    ins = dve.tensor_scalar(le[:, b, j, :], d_first[:, :], src4[:, bass.ds(t, 1)], 0.0,
                                            ALU.is_le, ALU.add, accum_out=above[:, bass.ds(t, 1)])
                ins.then_inc(v_le, 1)

            def count(c, u):
                U = c * UNITS + u
                need(dve, t_dq, U + 1)
                need(dve, v_cnt, U)
                for j in range(2):
                    t = c * C + (2 * u + j)
                    dve.tensor_scalar(hits[:, 2 * j, :], dq_ps[:, j * T:(j + 1) * T], src4[:, bass.ds(t, 1)], 0.0,
                                      ALU.is_le, ALU.add, accum_out=below[:, bass.ds(t, 1)])
                    ins = dve.tensor_scalar(hits[:, 2 * j + 1, :], dq_ps[:, j * T:(j + 1) * T], src4[:, bass.ds(t, 1)], 0.0,
                                            ALU.is_equal, ALU.add, accum_out=same[:, bass.ds(t, 1)])
                ins.then_inc(v_cnt, 1)

            def scan(at, c, stage):
                g = c + stage * 2 * LOOPS
                at.link(dve.tensor_copy(sc_in[:, :, 0], sc_out[:, :, C]))
                need(dve, a_mk, g + 1)
                if stage:
                    need(dve, a_S, g - 2 * LOOPS)
                dve.tensor_tensor_scan(sc_out[:, :, :].rearrange("p f t -> p (f t)"),
                                       mk[:, :, :].rearrange("p f t -> p (f t)"),
                                       sc_in[:, :, :].rearrange("p f t -> p (f t)"), 0.0, ALU.mult,
                                       ALU.add).then_inc(v_scan, 1)
                need(dve, v_scan, g + 1)

            sums = sc_out[:, :, 1:C + 1].rearrange("p f t -> p t f")

            base_A, K_A = at.n, 10
            compare(0, 0, 0)
            compare(0, 1, 0)
            with dve.Fori(0, LOOPS) as i:
                at = Steps(i * K_A + base_A)
                for s in range(2):
                    c = i * 2 + s
                    for u in range(UNITS):
                        count(c, u)
                        compare(c, u + 2, s)
                    need(dve, t_m, c * 2 + 2)
                    need(dve, v_scan, c)
                    dve.tensor_tensor(sc_in[:, :, 1:C + 1],
                                      m_ps[:, 0:C * D].rearrange("p (t f) -> p f t", f=D),
                                      b4r[:, :].rearrange("p (f o) -> p f o", o=1).broadcast_to([P, D, C]),
                                      ALU.add).then_inc(v_m, 1)
                    scan(at, c, 0)
                    cols = bass.ds(c * C, C)
                    cr = corr[:, 0:C, :]
                    at.link(dve.tensor_tensor(cr, sums, over_f(rcnt[:, cols], C), ALU.mult))
                    need(dve, a_xd, c + 1)
                    at.link(dve.tensor_tensor(cr, X1[:, cols, :], cr, ALU.add))
                    at.link(dve.tensor_reduce(st[:, 0, 0:C], cr, AX, ALU.add))
                    at.done(dve.scalar_tensor_tensor(out=X1[:, cols, :], in0=over_f(st[:, 0, 0:C], C),
                                                     scalar=-1.0 / D, in1=cr, op0=ALU.mult, op1=ALU.add))
                assert at.n == K_A, at.n
            end_A = base_A + K_A * LOOPS
            at = Steps(end_A)
            at.seen()
            carry(1, at)
            at.link(dve.tensor_reduce(st[:, 0, 0:1], car[:, 1, :], AX, ALU.add))
            dve.scalar_tensor_tensor(out=carc[:, :], in0=st[:, 0, 0:1].broadcast_to([P, D]), scalar=-1.0 / D,
                                     in1=car[:, 1, :], op0=ALU.mult, op1=ALU.add).then_inc(v_carc, 1)
            at.done(dve.tensor_scalar(tmp[:, :], same[:, :], 0.0, None, ALU.is_gt))
            at.link(dve.scalar_tensor_tensor(out=below[:, :], in0=above[:, 0:T], scalar=float(T), in1=below[:, :],
                                             op0=ALU.mult, op1=ALU.add))
            at.done(dve.tensor_tensor(w_eff[:, :], w[:, :], tmp[:, :], ALU.mult))
            at.link(dve.tensor_scalar(below[:, :], below[:, :], float(BIG - T - 1), None, ALU.add))
            dve.scalar_tensor_tensor(out=slot_i[:, :], in0=tmp[:, :], scalar=-float(BIG), in1=below[:, :],
                                     op0=ALU.mult, op1=ALU.add).then_inc(v_slot, 1)
            at.link(dve.memset(sc_out[:, :, C], 0.0))

            def norm_sum(at, rows, k, n, pn=P):
                at.link(dve.tensor_reduce(st[0:pn, k, 0:n], rows, AX, ALU.add))

            def centre(o, rows, k, n, pn=P):
                return dve.scalar_tensor_tensor(out=o, in0=over_f(st[0:pn, k, 0:n], n), scalar=-1.0 / D, in1=rows,
                                                op0=ALU.mult, op1=ALU.add)

            def norm_squares(sq, k, n, pn=P):
                return dve.tensor_reduce(st[0:pn, k, 0:n], sq, AX, ALU.add)

            def scaled(o, rows, k, n, pn=P):
                return dve.scalar_tensor_tensor(out=o, in0=rows, scalar=RT32, in1=over_f(st[0:pn, k, 0:n], n),
                                                op0=ALU.mult, op1=ALU.mult)

            def invert(at, k, n, pn=P):
                at.link(dve.reciprocal(st[0:pn, k, 0:n], st[0:pn, k, 0:n]))

            base = end_A + at.n

            def add_carry(i):
                Xc = X1[:, bass.ds(i * C2, C2), :]
                need(dve, p_corr, i + 1)
                dve.tensor_tensor(Xc, Xc, T1[:, bass.ds(i * C2, C2), :], ALU.add).then_inc(v_xc, 1)

            def make_y1(i, at):
                cols = bass.ds(i * C2, C2)
                need(dve, a_sq, i + 1)
                need(dve, v_y1, i)
                dve.tensor_reduce(st[:, 1, 0:C2], sqf[:, :, :], AX, ALU.add).then_inc(v_ss, 1)
                need(dve, a_sd, i + 1)
                at.link(dve.reciprocal(st[:, 1, 0:C2], st[:, 1, 0:C2]))
                dve.tensor_copy(rstd[:, cols], st[:, 1, 0:C2])
                at.link(dve.tensor_tensor(st[:, 2, 0:C2], st[:, 1, 0:C2], dinv[:, cols], ALU.mult))
                dve.scalar_tensor_tensor(out=T1[:, cols, :], in0=X1[:, cols, :], scalar=RT32,
                                         in1=over_f(st[:, 2, 0:C2], C2), op0=ALU.mult,
                                         op1=ALU.mult).then_inc(v_y1, 1)

            add_carry(0)
            with dve.Fori(0, LOOPS - 1) as i:
                add_carry(i + 1)
                at = Steps(i * 2 + base)
                make_y1(i, at)
            base += 2 * (LOOPS - 1)
            at = Steps(base)
            make_y1(LOOPS - 1, at)
            need(dve, v_y1, LOOPS)
            with dve.Fori(0, LOOPS) as i:
                cols = bass.ds(i * C2, C2)
                dve.scalar_tensor_tensor(out=X1[:, cols, :], in0=X1[:, cols, :], scalar=RT32,
                                         in1=over_f(rstd[:, cols], C2), op0=ALU.mult, op1=ALU.mult).then_inc(v_x1, 1)
            base += at.n

            def weigh(at, c, s, i, stage):
                dve.wait_ge(s_gy[s], (i + (1 + (stage - 1) * LOOPS)) * (16 * C))
                need(dve, v_scan, c + stage * 2 * LOOPS)
                dve.tensor_tensor(sc_in[:, :, 1:C + 1], y_ring[:, s, :, :].rearrange("p t f -> p f t"),
                                  w_eff[:, bass.ds(c * C, C)].rearrange("p (o t) -> p o t", o=1)
                                  .broadcast_to([P, D, C]), ALU.mult).then_inc(v_y, 1)
                scan(at, c, stage)
                if stage == 1:
                    cols = bass.ds(c * C, C)
                    at.done(dve.tensor_tensor(T1[:, cols, :], sums, over_f(ndinv2[:, cols], C), ALU.mult))

            def dense_centre(at, k, pn=P, rn=R):
                dve.wait_ge(s_xin, (k + 1) * 16)
                norm_sum(at, xin[0:pn, 0:rn, :], 3, rn, pn)
                centre(x1d[0:pn, 0:rn, :], xin[0:pn, 0:rn, :], 3, rn, pn).then_inc(v_dxc, 1)

            def dense_squares_1(k, pn=P, rn=R):
                need(dve, a_dsq, k + 1)
                norm_squares(sqd[0:pn, 0:rn, :], 4, rn, pn).then_inc(v_dss, 1)

            def dense_x1(at, k, pn=P, rn=R):
                need(dve, a_dsd, k + 1)
                invert(at, 4, rn, pn)
                scaled(x1d[0:pn, 0:rn, :], x1d[0:pn, 0:rn, :], 4, rn, pn).then_inc(v_dx1, 1)

            def dense_sum(at, k, w0, pn=P, rn=R, banks=BANKS):
                need(dve, v_dx1, k + 1)
                need(dve, v_od, k)
                for b, n in enumerate(banks):
                    need(dve, t_dh, w0 + b + 1)
                    r = 4 * sum(banks[0:b])
                    rows = x1d[0:pn, r:r + 4 * n, :]
                    dve.scalar_tensor_tensor(
                        out=rd[0:pn, r:r + 4 * n, :].rearrange("p a b -> p (a b)"),
                        in0=hd_ps[b % 2][0:pn, 0:n * P], scalar=0.0,
                        in1=rows.rearrange("p a b -> p (a b)"), op0=ALU.max, op1=ALU.add).then_inc(v_dh, 1)
                need(dve, v_dh, w0 + len(banks))
                norm_sum(at, rd[0:pn, 0:rn, :], 2, rn, pn)
                centre(rd[0:pn, 0:rn, :], rd[0:pn, 0:rn, :], 2, rn, pn).then_inc(v_dxc2, 1)

            def dense_squares_2(k, pn=P, rn=R):
                need(dve, a_dsq2, k + 1)
                norm_squares(od[0:pn, 0:rn, :], 5, rn, pn).then_inc(v_dss2, 1)

            def dense_out(at, k, pn=P, rn=R):
                need(dve, a_dsd2, k + 1)
                invert(at, 5, rn, pn)
                scaled(od[0:pn, 0:rn, :], rd[0:pn, 0:rn, :], 5, rn, pn).then_inc(v_od, 1)

            def both(at, i, k, stage, after=True, more=True):
                weigh(at, i * 2, 0, i, stage)
                dense_squares_1(k)
                if after:
                    dense_squares_2(k - 1)
                dense_x1(at, k)
                if after:
                    dense_out(at, k - 1)
                weigh(at, i * 2 + 1, 1, i, stage)
                dense_sum(at, k, k * 4)
                if more:
                    dense_centre(at, k + 1)
                else:
                    dense_centre(at, k + 1, TAILP, TAILR)

            at = Steps(base)
            dense_centre(at, 0)
            both(at, 0, 0, 1, after=False)
            base += at.n
            K_B = 8
            with dve.Fori(1, B_BOTH) as i:
                at = Steps((i - 1) * K_B + base)
                both(at, i, i, 1)
                assert at.n == K_B, at.n
            base += K_B * (B_BOTH - 1)
            at = Steps(base)
            weigh(at, 2 * LOOPS - 2, 0, LOOPS - 1, 1)
            dense_squares_2(B_BOTH - 1)
            dense_out(at, B_BOTH - 1)
            weigh(at, 2 * LOOPS - 1, 1, LOOPS - 1, 1)
            carry(2, at)
            at.link(dve.tensor_tensor(prer[:, :], pre[:, :], ndinv2[:, :], ALU.mult))
            base += at.n

            with dve.Fori(0, LOOPS) as i:
                at = Steps(i + base)
                cols = bass.ds(i * C2, C2)
                need(dve, v_y2, i)
                at.link(dve.tensor_tensor(corr[:, :, :], over_f(prer[:, cols], C2), over_t(car[:, 2, :], C2), ALU.mult))
                dve.tensor_tensor(T1[:, cols, :], T1[:, cols, :], corr[:, :, :], ALU.add).then_inc(v_y2, 1)
            base += LOOPS
            at = Steps(base)
            need(dve, a_S, 2 * LOOPS)
            at.link(dve.memset(sc_out[:, :, C], 0.0))

            dense_squares_1(B_BOTH)
            dense_x1(at, B_BOTH)
            dense_sum(at, B_BOTH, 4 * B_BOTH)
            dense_centre(at, B_BOTH + 1)
            base += at.n
            K_C = 6
            with dve.Fori(0, C_BOTH - 1) as i:
                at = Steps(i * K_C + base)
                both(at, i, i + (B_BOTH + 1), 2)
                assert at.n == K_C, at.n
            base += K_C * (C_BOTH - 1)
            at = Steps(base)
            both(at, C_BOTH - 1, NK - 1, 2, more=False)
            weigh(at, 2 * LOOPS - 2, 0, LOOPS - 1, 2)
            dense_squares_1(NK, TAILP, TAILR)
            dense_squares_2(NK - 1)
            dense_x1(at, NK, TAILP, TAILR)
            dense_out(at, NK - 1)
            dense_sum(at, NK, NK * 4, TAILP, TAILR, [1])
            dense_squares_2(NK, TAILP, TAILR)
            dense_out(at, NK, TAILP, TAILR)
            need(dve, v_od, NK + 1)
            for z in Z:
                at.link(dve.memset(z[:, :, 3 * D:4 * D], 0.0))
                dve.memset(z[:, :, 3 * D:3 * D + 1], 1.0).then_inc(v_const, 1)
            weigh(at, 2 * LOOPS - 1, 1, LOOPS - 1, 2)
            carry(3, at)
            base += at.n

            def z_rows(at, c, s):
                cols = bass.ds(c * C, C)
                zr = cz[:, 0:C, :]
                need(dve, v_z, c)
                at.link(dve.tensor_tensor(zr, over_f(pre[:, cols], C), over_t(car[:, 2, :], C), ALU.mult))
                at.link(dve.tensor_tensor(zr, S[:, cols, :], zr, ALU.add))
                at.link(dve.tensor_tensor(Z[s][:, :, D:2 * D], zr, over_f(ndinv[:, cols], C), ALU.mult))
                at.link(dve.tensor_tensor(zr, over_f(pre[:, cols], C), over_t(car[:, 3, :], C), ALU.mult))
                at.link(dve.tensor_tensor(zr, T1[:, cols, :], zr, ALU.add))
                dve.tensor_tensor(Z[s][:, :, 2 * D:3 * D], zr, over_f(n2dinv[:, cols], C), ALU.mult).then_inc(v_z, 1)

            def finish(at, c, s, more=True):
                if more:
                    z_rows(at, c + 1, 1 - s)
                cols = bass.ds(c * C, C)
                cr = corr[:, 0:C, :]
                need(dve, v_o, c)
                need(dve, t_hf, c * 4 + 4)
                dve.scalar_tensor_tensor(out=cr, in0=hf_ps[:, 0:C * D].rearrange("p (t f) -> p t f", f=D),
                                         scalar=0.0, in1=X1[:, cols, :], op0=ALU.max,
                                         op1=ALU.add).then_inc(v_fh, 1)
                need(dve, v_fh, c + 1)
                norm_sum(at, cr, 6, C)
                centre(cr, cr, 6, C).then_inc(v_fxc, 1)
                need(dve, a_fsq, c + 1)
                norm_squares(sqf[:, 0:C, :], 7, C).then_inc(v_fss, 1)
                need(dve, a_fsd, c + 1)
                invert(at, 7, C)
                need(dve, o_sc, c - 1)
                scaled(o_ring[:, s, :, :], cr, 7, C).then_inc(v_o, 1)

            at = Steps(base)
            z_rows(at, 0, 0)
            base += at.n
            K_F = 14
            with dve.Fori(0, LOOPS - 1) as i:
                at = Steps(i * K_F + base)
                finish(at, i * 2, 0)
                finish(at, i * 2 + 1, 1)
                assert at.n == K_F, at.n
            at = Steps(base + K_F * (LOOPS - 1))
            finish(at, 2 * LOOPS - 2, 0)
            finish(at, 2 * LOOPS - 1, 1, more=False)


_INS = ["x", "src", "dst", "edge_weight", "L0_gnn_W1", "L0_gnn_b1", "L0_gnn_W2", "L0_gnn_b2",
        "L0_gnn_W3", "L0_gnn_b3", "L0_gnn_W4", "L0_gnn_b4", "L1_gnn_W", "L1_gnn_b"]


def kernel(**inputs):
    import numpy as _np
    import concourse.bacc as _bacc
    from concourse import mybir as _mybir
    from concourse.bass_utils import run_bass_kernel_spmd as _run

    nc = _bacc.Bacc("TRN2", target_bir_lowering=False, num_devices=1)
    arrays, args = {}, []
    for name in _INS:
        a = _np.ascontiguousarray(inputs[name])
        arrays[f"in_{name}_dram"] = a
        args.append(nc.dram_tensor(f"in_{name}_dram", a.shape, _mybir.dt.from_np(a.dtype), kind="ExternalInput").ap())
    shape = inputs["x"].shape
    o = nc.dram_tensor("out_0_dram", shape, _mybir.dt.float32, kind="ExternalOutput").ap()
    build(nc, *args, o)
    r = _run(nc, [arrays], core_ids=[0])
    return r.results[0]["out_0_dram"]
```

```python
from contextlib import ExitStack

import concourse.bass as bass
from concourse import mybir

ALU = mybir.AluOpType
ACT = mybir.ActivationFunctionType
AX = mybir.AxisListType.X
F32 = mybir.dt.float32
I32 = mybir.dt.int32
F16 = mybir.dt.float16
BF16 = mybir.dt.bfloat16

P = 128
BIG = 1 << 20
PAD = (1 << 17) - 4
EPS = 1e-5
OFF = 2


def build(nc, x, src, dst, edge_weight, W1, b1, W2, b2, W3, b3, W4, b4, Wc, bc, out):
    N, D = x.shape
    E = src.shape[0]
    H1, H2, H3 = W1.shape[1], W2.shape[1], W3.shape[1]
    C = 14
    T = -(-E // (P * 2 * C)) * 2 * C
    LOOPS = T // (2 * C)
    FULL, REM = E // T, E % T
    PAIRS = [4, 3]
    UNITS = C // 2
    C2 = 2 * C
    R = 60
    NK = 13
    TAILP, TAILR = 40, 4
    assert P * R * NK + TAILP * TAILR == N and 2 * D == H1 and sum(PAIRS) == UNITS
    BANKS = [4, 4, 4, 3]
    FBANKS = [4, 4, 4, 2]
    IDLE_FILL = 3
    BROWS = 96
    RT32 = float(D) ** 0.5
    B_BOTH = LOOPS - 1
    C_BOTH = NK - B_BOTH - 2

    ctx = ExitStack()
    with ctx:
        def sb(name, shape, dt=F32):
            return ctx.enter_context(nc.sbuf_tensor(name, shape, dt))

        def sem(name):
            return ctx.enter_context(nc.semaphore(name))

        dst_x = sb("dst_x", [P, T + 2], I32)
        dst_up = sb("dst_up", [P, T], I32)
        src_i = sb("src_i", [P, T], I32)
        w = sb("w", [P, T])
        dst1 = sb("dst1", [P, T + 2])
        src4 = sb("src4", [P, T + 4])
        d_first = sb("d_first", [P, P])
        d_diff = sb("d_diff", [P, T])
        d_delta = sb("d_delta", [P, 2, T], F16)
        cont = sb("cont", [P, T])
        last = sb("last", [P, T])
        pre = sb("pre", [P, T])
        cnt = sb("cnt", [P, T])
        rcnt = sb("rcnt", [P, T])
        joint = sb("joint", [P, T])
        j_scal = sb("j_scal", [P, 3, 1])
        j_rstd = sb("j_rstd", [P, 1])
        j_hits = sb("j_hits", [P, T])
        j_i = sb("j_i", [P, 1], I32)
        j_scat = sb("j_scat", [P, 1], I32)
        deg = sb("deg", [P, T])
        dinv = sb("dinv", [P, T])
        ndinv = sb("ndinv", [P, T])
        ndinv2 = sb("ndinv2", [P, T])
        n2dinv = sb("n2dinv", [P, T])
        above = sb("above", [P, T + 4])
        below = sb("below", [P, T])
        same = sb("same", [P, T])
        w_eff = sb("w_eff", [P, T])
        tmp = sb("tmp", [P, T])
        hits = sb("hits", [P, 4, T])
        ones = sb("ones", [P, T])
        epsc = sb("epsc", [P, 1])
        zeros = sb("zeros", [P, T])
        slot_i = sb("slot_i", [P, T], I32)
        scat_i = sb("scat_i", [P, T], I32)
        X1 = sb("X1", [P, T, D])
        S = sb("S", [P, T, D])
        T1 = sb("T1", [P, T, D])
        x_ring = sb("x_ring", [P, 2, C, 2 * D])
        y_ring = sb("y_ring", [P, 2, C, D])
        o_ring = sb("o_ring", [P, 2, C, D])
        di_ring = sb("di_ring", [P, 2, C], I32)
        si_ring = sb("si_ring", [P, 2, C], I32)
        mk = sb("mk", [P, D, C + 1])
        sc_in = sb("sc_in", [P, D, C + 1])
        sc_out = sb("sc_out", [P, D, C + 1])
        corr = sb("corr", [P, C2, D])
        cz = sb("cz", [P, C, D])
        diag = sb("diag", [P, P])
        xT = sb("xT", [P, 512])
        h1 = sb("h1", [P, 512])
        h2 = sb("h2", [P, 2, 512])
        h3 = sb("h3", [P, 512])
        le = sb("le", [P, 2, 2, P], F16)
        leT = sb("leT", [P, 2, 2 * P], F16)
        w1s = sb("w1s", [P, P])
        w1b = sb("w1b", [P, P])
        w2s = sb("w2s", [P, 2, H2])
        w3s = sb("w3s", [P, 2, P])
        w4s = sb("w4s", [P, 2 * D])
        b1c = sb("b1c", [P, 1])
        b2c = sb("b2c", [P, 1])
        b3c = sb("b3c", [P, 1])
        b4r = sb("b4r", [P, D])
        ident = sb("ident", [P, P])
        ident16 = sb("ident16", [P, P], F16)
        wd = sb("wd", [P, P])
        wd2 = sb("wd2", [P, P])
        wf = sb("wf", [P, D])
        wf2 = sb("wf2", [D, D])
        brow = sb("brow", [BROWS, 512])
        b_near = sb("b_near", [BROWS, 512], BF16)
        b_parts = sb("b_parts", [BROWS, 512], BF16)
        onerow = sb("onerow", [BROWS, P], BF16)
        tails = sb("tails", [P, D])
        spans = sb("spans", [P, D])
        rstd = sb("rstd", [P, T])
        j_old = sb("j_old", [P, D])
        j_new = sb("j_new", [P, D])
        j_sums = sb("j_sums", [P, 2, D])
        j_parts = sb("j_parts", [P, 2, D])
        j_out = sb("j_out", [P, D])
        j_part = sb("j_part", [P, D])
        j_sq = sb("j_sq", [P, D])
        j_y1 = sb("j_y1", [P, D])
        j_y2 = sb("j_y2", [P, D])
        j_row = sb("j_row", [P, D])
        tailT = sb("tailT", [D, P])
        spanT = sb("spanT", [D, P])
        carT = sb("carT", [D, P])
        car = sb("car", [P, 4, D])
        carc = sb("carc", [P, D])
        xin = sb("xin", [P, R, D])
        x1d = sb("x1d", [P, R, D])
        sqd = sb("sqd", [P, R, D])
        rd = sb("rd", [P, R, D])
        od = sb("od", [P, R, D])
        x1T = sb("x1T", [P, 2, 512])
        st = sb("st", [P, 8, R])
        Z = [a[:, :, :].rearrange("p r f -> p (r f)")[:, 0:C * 4 * D].rearrange("p (t f) -> p t f", f=4 * D)
             for a in (xin, x1d)]
        ZT = sb("ZT", [P, 2, 512])
        sqf = sb("sqf", [P, C2, D])

        bank = [ctx.enter_context(nc.psum_tensor(f"bank{i}", [P, 512], F32)) for i in range(8)]
        leT16_ps = bank[6][:, :].bitcast(F16)
        xT_ps, h1_ps, h3_ps, m_ps, dq_ps = (bank[i] for i in (0, 1, 4, 5, 7))
        h2_ps = [bank[2], bank[3]]
        car_ps = bank[6]
        x1T_ps = [bank[0], bank[1]]
        hd_ps = [bank[2], bank[3]]
        ZT_ps = [bank[4], bank[5]]
        hf_ps = bank[7]

        y1_dram = nc.dram_tensor("y1_by_slot", [P * T, D], F32, kind="Internal").ap()
        y2_dram = nc.dram_tensor("y2_by_slot", [P * T, D], F32, kind="Internal").ap()

        s_nodes = sem("s_nodes")
        s_edges = sem("s_edges")
        s_wts = sem("s_wts")
        s_gx = [[sem(f"s_gx{i}_part{v}") for v in range(2)] for i in range(2)]
        s_gy = [sem(f"s_gy{i}") for i in range(2)]
        s_sc = [sem(f"s_sc{i}") for i in range(2)]
        s_y1 = sem("s_y1")
        s_y2 = sem("s_y2")
        s_xin = sem("s_xin")
        s_od = sem("s_od")
        o_od = sem("o_od")
        o_sc = sem("o_sc")
        p_id = sem("p_id")
        p_idx = sem("p_idx")
        p_begun = sem("p_begun")
        v_fill = sem("v_fill")
        v_rings = sem("v_rings")
        v_scan = sem("v_scan")
        v_j1 = sem("v_j1")
        v_j2 = sem("v_j2")
        v_jss = sem("v_jss")
        a_jsd = sem("a_jsd")
        s_j1 = sem("s_j1")
        s_jg = sem("s_jg")
        s_jo = sem("s_jo")
        v_jz = sem("v_jz")
        t_jz = sem("t_jz")
        a_jz = sem("a_jz")
        t_jh = sem("t_jh")
        v_jo = sem("v_jo")
        s_j2 = sem("s_j2")
        v_const = sem("v_const")
        a_mk = sem("a_mk")
        a_S = sem("a_S")
        v_deg = sem("v_deg")
        v_ss = sem("v_ss")
        v_dss = sem("v_dss")
        v_dss2 = sem("v_dss2")
        v_fss = sem("v_fss")
        v_pad = sem("v_pad")
        v_wts = sem("v_wts")
        v_diag = sem("v_diag")
        v_tail = sem("v_tail")
        v_ct = sem("v_ct")
        v_le = sem("v_le")
        v_cnt = sem("v_cnt")
        v_m = sem("v_m")
        v_slot = sem("v_slot")
        v_y = sem("v_y")
        v_idx = sem("v_idx")
        v_di = sem("v_di")
        v_y1 = sem("v_y1")
        v_y2 = sem("v_y2")
        v_dxc = sem("v_dxc")
        v_dx1 = sem("v_dx1")
        v_dh = sem("v_dh")
        v_dxc2 = sem("v_dxc2")
        v_od = sem("v_od")
        v_z = sem("v_z")
        v_fh = sem("v_fh")
        v_fxc = sem("v_fxc")
        v_o = sem("v_o")
        v_step = sem("v_step")
        t_d0 = sem("t_d0")
        t_tail = sem("t_tail")
        t_ct = sem("t_ct")
        t_leT = sem("t_leT")
        t_dq = sem("t_dq")
        t_xT = sem("t_xT")
        t_h1 = sem("t_h1")
        t_h2 = sem("t_h2")
        t_h3 = sem("t_h3")
        t_m = sem("t_m")
        t_dT = sem("t_dT")
        t_dh = sem("t_dh")
        t_ZT = sem("t_ZT")
        t_hf = sem("t_hf")
        a_deg = sem("a_deg")
        a_sd = sem("a_sd")
        a_dsd = sem("a_dsd")
        a_dsd2 = sem("a_dsd2")
        a_fsd = sem("a_fsd")
        a_leT = sem("a_leT")
        a_xT = sem("a_xT")
        a_h1 = sem("a_h1")
        a_h2 = sem("a_h2")
        a_h3 = sem("a_h3")
        a_xd = sem("a_xd")
        a_idx = sem("a_idx")
        a_dsq = sem("a_dsq")
        a_dT = sem("a_dT")
        a_dsq2 = sem("a_dsq2")
        a_z = sem("a_z")
        a_ZT = sem("a_ZT")
        a_fsq = sem("a_fsq")

        def need(eng, s, n):
            eng.wait_ge(s, n + OFF)

        def over_f(a, n):
            return a.rearrange("p (n o) -> p n o", o=1).broadcast_to([a.shape[0], n, D])

        y1_st = y1_dram.rearrange("(p t) f -> p t f", p=P)
        y2_st = y2_dram.rearrange("(p t) f -> p t f", p=P)
        x_d = x[0:P * R * NK, :].rearrange("(p r) f -> p r f", p=P)
        out_d = out[0:P * R * NK, :].rearrange("(p r) f -> p r f", p=P)
        x_tail = x[P * R * NK:N, :].rearrange("(p r) f -> p r f", r=TAILR)
        out_tail = out[P * R * NK:N, :].rearrange("(p r) f -> p r f", r=TAILR)

        NODE_DMAS, EDGE_DMAS = 4, 6
        WT_DMAS = 32
        block = ctx.enter_context(nc.Block())

        @block.sync
        def _(sp):
            def edge_rows(a, s0, n, m):
                return a[s0:s0 + n * T].rearrange("(p t) -> p t", t=T)[:, 0:m] if n > 1 else \
                    a[s0:s0 + m].rearrange("(p t) -> p t", p=1)

            sp.sem_inc(o_od, OFF)
            sp.sem_inc(o_sc, OFF)
            sp.wait_ge(v_pad, 4)
            sp.dma_start(dst_x[0:FULL, 1:T + 1], edge_rows(dst, 0, FULL, T)).then_inc(s_nodes, 16)
            sp.dma_start(dst_x[FULL:P, 1:REM + 1], edge_rows(dst, FULL * T, 1, REM)).then_inc(s_nodes, 16)
            sp.dma_start(src_i[0:FULL, :], edge_rows(src, 0, FULL, T)).then_inc(s_nodes, 16)
            sp.dma_start(src_i[FULL:P, 0:REM], edge_rows(src, FULL * T, 1, REM)).then_inc(s_nodes, 16)
            sp.dma_start(w[0:FULL, :], edge_rows(edge_weight, 0, FULL, T)).then_inc(s_edges, 16)
            sp.dma_start(w[FULL:P, 0:REM], edge_rows(edge_weight, FULL * T, 1, REM)).then_inc(s_edges, 16)
            sp.dma_start(dst_up[1:P, :], edge_rows(dst, 0, FULL, T)).then_inc(s_edges, 16)
            with nc.allow_non_contiguous_dma(reason="one neighbour for each partition"):
                sp.dma_start(dst_x[1:P, 0:1], edge_rows(dst, 0, FULL, T)[:, T - 1:T]).then_inc(s_edges, 16)
                sp.dma_start(dst_x[0:FULL - 1, T + 1:T + 2],
                             edge_rows(dst, T, FULL - 1, T)[:, 0:1]).then_inc(s_edges, 16)
                sp.dma_start(dst_x[FULL - 1:FULL, T + 1:T + 2],
                             edge_rows(dst, FULL * T, 1, 1)).then_inc(s_edges, 16)

            sp.wait_ge(v_fill, 8)

            def wt(o, i):
                sp.dma_start(o, i).then_inc(s_wts, 16)

            for g in range(2):
                h = g * H1
                wt(w1s[h:h + D, h:h + H1], W1[0:D, :])
                wt(w1s[h + D:h + 2 * D, h:h + H1], W1[D:2 * D, :])
                wt(w1b[h:h + D, h:h + H1], W1[D:2 * D, :])
                wt(w2s[h:h + H1, g, :], W2[:, :])
                wt(w3s[:, g, h:h + H3], W3[:, :])
                wt(w4s[h:h + H3, g * D:(g + 1) * D], W4[:, :])
                wt(b1c[h:h + H1, :], b1.rearrange("(p o) -> p o", o=1))
                wt(b3c[h:h + H3, :], b3.rearrange("(p o) -> p o", o=1))
            wt(b2c[:, :], b2.rearrange("(p o) -> p o", o=1))
            wt(b4r[:, :], b4.rearrange("(o f) -> o f", o=1).broadcast_to([P, D]))
            for g in range(4):
                h = g * D
                wt(wd[h:h + D, h:h + D], Wc[0])
                wt(wd2[h:h + D, h:h + D], Wc[2])
            wt(wf[0:D, :], Wc[0])
            wt(wf2[:, :], Wc[2])
            wt(wf[D:2 * D, :], Wc[1])
            wt(wf[2 * D:3 * D, :], Wc[2])
            wt(wf[3 * D:3 * D + 1, :], bc.rearrange("(o f) -> o f", o=1))
            wt(brow.rearrange("o (r f) -> o r f", f=D),
               bc.rearrange("(o r f) -> o r f", o=1, r=1).broadcast_to([BROWS, 512 // D, D]))

            sp.dma_start(xin[:, :, :], x_d[:, 0:R, :]).then_inc(s_xin, 16)
            with sp.Fori(0, 2 * LOOPS) as c:
                need(sp, v_y1, c + 1)
                sp.dma_start(y1_st[:, bass.ds(c * C, C), :], T1[:, bass.ds(c * C, C), :]).then_inc(s_y1, 16)

            def load(k):
                need(sp, v_dxc, k)
                sp.dma_start(xin[:, :, :], x_d[:, bass.ds(k * R, R), :]).then_inc(s_xin, 16)

            def store(k):
                need(sp, v_od, k + 1)
                sp.dma_start(out_d[:, bass.ds(k * R, R), :], od[:, :, :]).then_inc(s_od, 16)

            def stored(k):
                sp.wait_ge(s_od, (k + 1) * 16)
                sp.sem_inc(o_od)

            def store_y2(c):
                need(sp, v_y2, c + 1)
                sp.dma_start(y2_st[:, bass.ds(c * C, C), :], T1[:, bass.ds(c * C, C), :]).then_inc(s_y2, 16)

            load(1)
            with sp.Fori(0, LOOPS - 1) as i:
                load(i + 2)
                store_y2(i * 2)
                store(i)
                store_y2(i * 2 + 1)
                stored(i)
            load(LOOPS + 1)
            store_y2(2 * LOOPS - 2)
            store_y2(2 * LOOPS - 1)
            sp.wait_ge(s_j2, 16)
            store(LOOPS - 1)
            stored(LOOPS - 1)
            with sp.Fori(LOOPS + 1, NK - 1) as k:
                load(k + 1)
                store(k - 1)
                stored(k - 1)
            need(sp, v_dxc, NK)
            sp.dma_start(xin[0:TAILP, 0:TAILR, :], x_tail).then_inc(s_xin, 16)
            for k in (NK - 2, NK - 1):
                store(k)
                stored(k)
            need(sp, v_od, NK + 1)
            sp.dma_start(out_tail, od[0:TAILP, 0:TAILR, :]).then_inc(s_od, 16)
            sp.wait_ge(s_od, 16 * (NK + 1))

            with sp.Fori(0, LOOPS) as i:
                for s in range(2):
                    sp.wait_ge(s_sc[s], (i + 1) * (16 * C))
                    sp.sem_inc(o_sc)

        @block.gpsimd
        def _(pool):
            top_node = pool.to_reg(N - 1)
            top_slot = pool.to_reg(P * T - 1)
            nc.gpsimd.memset(ident[:, :], 0.0).then_inc(p_id, 1)
            pool.wait_ge(p_id, 1)
            nc.gpsimd.affine_select(out=ident[:, :], in_=ident[:, :], compare_op=ALU.not_equal, fill=1.0,
                                    base=0, pattern=[[-1, P]], channel_multiplier=1).then_inc(p_id, 1)

            def rows(s, ring, table, idx, k, top, done):
                nc.gpsimd.indirect_dma_start(
                    out=ring, out_offset=None, in_=table,
                    in_offset=bass.IndirectOffsetOnAxis(ap=idx[:, s, k:k + 1], axis=0),
                    bounds_check=top, oob_is_err=False).then_inc(done, 16)

            pool.wait_ge(s_nodes, 16 * NODE_DMAS)
            pool.wait_ge(v_rings, 2)

            def two(a):
                return a.rearrange("p (s t) -> p s t", s=2)

            nc.gpsimd.tensor_copy(di_ring[:, :, :], two(dst_x[:, 1:C2 + 1])).then_inc(p_idx, 1)
            nc.gpsimd.tensor_copy(si_ring[:, :, :], two(src_i[:, 0:C2])).then_inc(p_idx, 1)
            pool.wait_ge(p_idx, 2)
            with pool.Fori(0, LOOPS) as i:
                for s in range(2):
                    c = i * 2 + s
                    need(pool, a_idx, c - 1)
                    need(pool, a_xd, c - 1)
                    pool.sem_inc(p_begun)
                    for k in range(C):
                        done = s_gx[s][k // (2 * PAIRS[0])]
                        rows(s, x_ring[:, s, k, 0:D], x[:, :], di_ring, k, top_node, done)
                        rows(s, x_ring[:, s, k, D:2 * D], x[:, :], si_ring, k, top_node, done)

            def put_joints(table, rows_at_joints, done):
                nc.gpsimd.indirect_dma_start(
                    out=table[:, :], out_offset=bass.IndirectOffsetOnAxis(ap=j_i[:, 0:1], axis=0),
                    in_=rows_at_joints[:, :], in_offset=None,
                    bounds_check=top_slot, oob_is_err=False).then_inc(done, 16)
                pool.wait_ge(done, 16)

            for stage, table in enumerate((y1_dram, y2_dram)):
                if stage == 0:
                    pool.wait_ge(v_slot, 1)
                    pool.wait_ge(s_y1, 16 * 2 * LOOPS)
                    pool.wait_ge(v_j1, 1)
                    put_joints(y1_dram, j_y1, s_j1)
                else:
                    pool.wait_ge(s_y2, 16 * 2 * LOOPS)
                    nc.gpsimd.indirect_dma_start(
                        out=j_row[:, :], out_offset=None, in_=y2_dram[:, :],
                        in_offset=bass.IndirectOffsetOnAxis(ap=j_i[:, 0:1], axis=0),
                        bounds_check=top_slot, oob_is_err=False).then_inc(s_jg, 16)
                    pool.wait_ge(v_j2, 1)
                    put_joints(y2_dram, j_y2, s_j2)
                nc.gpsimd.tensor_copy(si_ring[:, :, :], two(slot_i[:, 0:C2])).then_inc(p_idx, 1)
                pool.wait_ge(p_idx, 3 + stage)
                with pool.Fori(0, LOOPS) as i:
                    for s in range(2):
                        c = i * 2 + s
                        need(pool, v_idx, c - 1 + stage * (2 * LOOPS - 2))
                        need(pool, v_y, c - 1 + stage * 2 * LOOPS)
                        pool.sem_inc(p_begun)
                        for k in range(C):
                            rows(s, y_ring[:, s, k, :], table[:, :], si_ring, k, top_slot, s_gy[s])

            pool.wait_ge(s_od, 16 * (NK + 1))
            with pool.Fori(0, LOOPS) as i:
                for s in range(2):
                    c = i * 2 + s
                    need(pool, v_di, c + 1)
                    need(pool, v_o, c + 1)
                    pool.sem_inc(p_begun)
                    for k in range(C):
                        nc.gpsimd.indirect_dma_start(
                            out=out[:, :], out_offset=bass.IndirectOffsetOnAxis(ap=di_ring[:, s, k:k + 1], axis=0),
                            in_=o_ring[:, s, k, :], in_offset=None,
                            bounds_check=top_node, oob_is_err=False).then_inc(s_sc[s], 16)
            pool.wait_ge(v_jo, 1)
            nc.gpsimd.indirect_dma_start(
                out=out[:, :], out_offset=bass.IndirectOffsetOnAxis(ap=j_scat[:, 0:1], axis=0),
                in_=j_out[:, :], in_offset=None, bounds_check=top_node, oob_is_err=False).then_inc(s_jo, 16)
            for s in range(2):
                pool.wait_ge(s_sc[s], 16 * C * LOOPS)
            pool.wait_ge(s_jo, 16)

        @block.tensor
        def _(pe):
            for q in (t_leT, t_dq, t_xT, t_h1, t_h2, t_h3, t_m, t_dT, t_dh, t_ZT, t_hf):
                pe.sem_inc(q, OFF)
            pe.wait_ge(p_id, 2)

            def carry(k):
                pe.wait_ge(v_tail, k + 1)
                ins = pe.transpose(car_ps[0:D, 0:P], tails[:, :], ident[:, :])
                if k == 0:
                    ins = pe.transpose(car_ps[0:D, P:2 * P], spans[:, :], ident[:, :])
                ins.then_inc(t_tail, 1)
                pe.wait_ge(v_ct, k + 1)
                pe.transpose(car_ps[:, 2 * P:2 * P + D], carT[:, :], ident[0:D, 0:D]).then_inc(t_ct, 1)

            pe.wait_ge(v_diag, 1)
            pe.matmul(dq_ps[:, 0:P], ones[:, 0:P], diag[:, :], start=True, stop=True).then_inc(t_d0, 1)
            carry(0)

            def look_T(c, u, s):
                U, b = c * UNITS + u, (s + u) % 2
                need(pe, v_le, U + 1)
                need(pe, a_leT, U)
                for j in range(2):
                    ins = pe.transpose(leT16_ps[:, j * P:(j + 1) * P], le[:, b, j, :], ident16[:, :])
                ins.then_inc(t_leT, 1)

            def look_D(c, u, s):
                U, b = c * UNITS + u, (s + u) % 2
                need(pe, a_leT, U + 1)
                need(pe, v_cnt, U)
                for j in range(2):
                    for part in range(2):
                        ins = pe.matmul(dq_ps[:, j * T:(j + 1) * T], leT[:, b, j * P:(j + 1) * P],
                                        d_delta[:, part, :], start=(part == 0), stop=(part == 1))
                ins.then_inc(t_dq, 1)

            def mlp_T(i, c, v, s):
                pe.wait_ge(s_gx[s][v], (i + 1) * (64 * PAIRS[v]))
                need(pe, a_xT, c * 2 + v)
                for q in range(PAIRS[v]):
                    t = 2 * (q + v * PAIRS[0])
                    ins = pe.transpose(xT_ps[:, q * P:(q + 1) * P],
                                       x_ring[:, s, t:t + 2, :].rearrange("p a b -> p (a b)"), ident[:, :])
                ins.then_inc(t_xT, 1)

            def mlp_1(c, v):
                n = PAIRS[v] * P
                need(pe, a_xT, c * 2 + v + 1)
                need(pe, a_h1, c * 2 + v)
                pe.matmul(h1_ps[:, 0:n], w1s[:, :], xT[:, 0:n], start=True, stop=True).then_inc(t_h1, 1)

            def mlp_2(c, v):
                n = PAIRS[v] * P
                need(pe, a_h1, c * 2 + v + 1)
                for g in range(2):
                    need(pe, a_h2, c * 4 + 2 * v + g - 1)
                    pe.matmul(h2_ps[g][:, 0:n], w2s[:, g, :], h1[:, 0:n], start=True, stop=True).then_inc(t_h2, 1)

            def mlp_3(c, v):
                n = PAIRS[v] * P
                need(pe, a_h2, c * 4 + 2 * v + 2)
                need(pe, a_h3, c * 2 + v)
                for g in range(2):
                    ins = pe.matmul(h3_ps[:, 0:n], w3s[:, g, :], h2[:, g, 0:n], start=(g == 0), stop=(g == 1))
                ins.then_inc(t_h3, 1)

            def mlp_4(c, v):
                need(pe, a_h3, c * 2 + v + 1)
                if v == 0:
                    need(pe, v_m, c)
                for q in range(PAIRS[v]):
                    g = q + v * PAIRS[0]
                    ins = pe.matmul(m_ps[:, g * 2 * D:(g + 1) * 2 * D], h3[:, q * P:(q + 1) * P], w4s[:, :],
                                    start=True, stop=True)
                ins.then_inc(t_m, 1)

            def look(c, j, s):
                if j < UNITS:
                    look_T(c, j, s)
                if j > 0:
                    look_D(c, j - 1, s)

            def chunk_A(i, c, s):
                look(c + 1, 0, 1 - s)
                mlp_T(i, c, 0, s)
                look(c + 1, 1, 1 - s)
                mlp_1(c, 0)
                look(c + 1, 2, 1 - s)
                mlp_2(c, 0)
                mlp_T(i, c, 1, s)
                look(c + 1, 3, 1 - s)
                mlp_3(c, 0)
                mlp_1(c, 1)
                look(c + 1, 4, 1 - s)
                mlp_4(c, 0)
                mlp_2(c, 1)
                look(c + 1, 5, 1 - s)
                mlp_3(c, 1)
                look(c + 1, 6, 1 - s)
                look(c + 1, 7, 1 - s)
                mlp_4(c, 1)

            for j in range(UNITS + 1):
                look(0, j, 0)
            pe.wait_ge(v_wts, 1)
            with pe.Fori(0, LOOPS - 1) as i:
                chunk_A(i, i * 2, 0)
                chunk_A(i, i * 2 + 1, 1)
            chunk_A(LOOPS - 1, 2 * LOOPS - 2, 0)

            need(pe, v_cnt, 2 * LOOPS * UNITS)

            def stay_awake():
                for _ in range(IDLE_FILL):
                    pe.matmul(dq_ps[:, 0:512], onerow[:, :], b_parts[:, :], start=True, stop=True)

            for v in range(2):
                mlp_T(LOOPS - 1, 2 * LOOPS - 1, v, 1)
                stay_awake()
                mlp_1(2 * LOOPS - 1, v)
                stay_awake()
                mlp_2(2 * LOOPS - 1, v)
                stay_awake()
                mlp_3(2 * LOOPS - 1, v)
                stay_awake()
                mlp_4(2 * LOOPS - 1, v)
            carry(1)

            def dense(k, banks, pn, w0):
                def turn(b):
                    need(pe, a_dT, w0 + b - 1)
                    for g in range(banks[b]):
                        r = 4 * (g + sum(banks[0:b]))
                        ins = pe.transpose(x1T_ps[b % 2][:, g * P:g * P + pn],
                                           x1d[0:pn, r:r + 4, :].rearrange("p a b -> p (a b)"),
                                           ident[0:pn, 0:pn])
                    ins.then_inc(t_dT, 1)

                need(pe, v_dx1, k + 1)
                turn(0)
                for b in range(len(banks)):
                    if b + 1 < len(banks):
                        turn(b + 1)
                    n = banks[b]
                    need(pe, a_dT, w0 + b + 1)
                    need(pe, v_dh, w0 + b - 1)
                    pe.matmul(hd_ps[b % 2][0:pn, 0:n * P], onerow[:, 0:pn], b_parts[:, 0:n * P], start=True, stop=False,
                              skip_group_check=True)
                    for g in range(n):
                        ins = pe.matmul(hd_ps[b % 2][0:pn, g * P:(g + 1) * P], x1T[:, b % 2, g * P:g * P + pn],
                                        wd[:, :], start=False, stop=(g == n - 1), skip_group_check=True)
                    ins.then_inc(t_dh, 1)

            with pe.Fori(0, B_BOTH + 1) as k:
                dense(k, BANKS, P, k * 4)
            carry(2)
            with pe.Fori(B_BOTH + 1, NK) as k:
                dense(k, BANKS, P, k * 4)
            dense(NK, [1], TAILP, NK * 4)

            def finish(c, s):
                need(pe, v_z, c + 1)
                need(pe, a_z, c + 1)
                need(pe, v_fh, c)

                def turn(b):
                    need(pe, a_ZT, c * 4 + b - 1)
                    for g in range(FBANKS[b]):
                        ins = pe.transpose(ZT_ps[b % 2][:, g * P:(g + 1) * P], Z[s][:, g + 4 * b, :], ident[:, :])
                    ins.then_inc(t_ZT, 1)

                turn(0)
                for b in range(4):
                    if b < 3:
                        turn(b + 1)
                    need(pe, a_ZT, c * 4 + b + 1)
                    for g in range(FBANKS[b]):
                        t = g + 4 * b
                        ins = pe.matmul(hf_ps[:, t * D:(t + 1) * D], ZT[:, b % 2, g * P:(g + 1) * P], wf[:, :],
                                        start=True, stop=True)
                    ins.then_inc(t_hf, 1)

            finish(0, 0)
            finish(1, 1)
            carry(3)
            with pe.Fori(1, LOOPS) as i:
                finish(i * 2, 0)
                finish(i * 2 + 1, 1)
            pe.wait_ge(v_jz, 1)
            need(pe, a_ZT, 2 * LOOPS * 4)
            pe.transpose(ZT_ps[0][:, 0:P], Z[0][:, 0, :], ident[:, :]).then_inc(t_jz, 1)
            pe.wait_ge(a_jz, 1)
            pe.matmul(hf_ps[:, 0:D], ZT[:, 0, 0:P], wf[:, :], start=True, stop=True).then_inc(t_jh, 1)

        @block.scalar
        def _(act):
            for q in (a_leT, a_xT, a_h1, a_h2, a_h3, a_xd, a_idx, a_dsq, a_dT, a_dsq2, a_z, a_ZT, a_fsq,
                      a_sd, a_dsd, a_dsd2, a_fsd, a_mk, a_S):
                act.sem_inc(q, OFF)
            act.wait_ge(v_deg, 1)
            nc.scalar.activation(dinv[:, :], dinv[:, :], ACT.Sqrt).then_inc(a_deg, 1)
            act.wait_ge(v_fill, 9)

            def deviation(ss, n, pn=P):
                return nc.scalar.activation(st[0:pn, ss, 0:n], st[0:pn, ss, 0:n], ACT.Sqrt, bias=epsc[0:pn, 0:1])

            def look(c, u, s):
                U, b = c * UNITS + u, (s + u) % 2
                need(act, t_leT, U + 1)
                need(act, t_dq, U - 1)
                nc.scalar.copy(leT[:, b, :], leT16_ps[:, 0:2 * P]).then_inc(a_leT, 1)

            def x_T(c, v):
                n = PAIRS[v] * P
                need(act, t_xT, c * 2 + v + 1)
                need(act, t_h1, c * 2 + v)
                nc.scalar.copy(xT[:, 0:n], xT_ps[:, 0:n]).then_inc(a_xT, 1)

            def relu_1(c, v):
                n = PAIRS[v] * P
                need(act, t_h1, c * 2 + v + 1)
                need(act, t_h2, c * 4 + 2 * v)
                nc.scalar.activation(h1[:, 0:n], h1_ps[:, 0:n], ACT.Relu, bias=b1c[:, 0:1]).then_inc(a_h1, 1)

            def relu_2(c, v):
                n = PAIRS[v] * P
                need(act, t_h3, c * 2 + v)
                for g in range(2):
                    need(act, t_h2, c * 4 + 2 * v + g + 1)
                    nc.scalar.activation(h2[:, g, 0:n], h2_ps[g][:, 0:n], ACT.Relu, bias=b2c[:, 0:1]).then_inc(a_h2, 1)

            def relu_3(c, v):
                n = PAIRS[v] * P
                need(act, t_h3, c * 2 + v + 1)
                need(act, t_m, c * 2 + v)
                nc.scalar.activation(h3[:, 0:n], h3_ps[:, 0:n], ACT.Relu, bias=b3c[:, 0:1]).then_inc(a_h3, 1)

            def spread_mask(c, stage):
                need(act, v_scan, c + stage * 2 * LOOPS)
                nc.scalar.copy(mk[:, :, 1:C + 1],
                               cont[:, bass.ds(c * C, C)].rearrange("p (o t) -> p o t", o=1)
                               .broadcast_to([P, D, C])).then_inc(a_mk, 1)

            def keep_sums(c, stage):
                need(act, v_scan, c + stage * 2 * LOOPS + 1)
                o = (S, T1)[stage - 1]
                nc.scalar.copy(o[:, bass.ds(c * C, C), :],
                               sc_out[:, :, 1:C + 1].rearrange("p f t -> p t f")).then_inc(a_S, 1)

            def keep_x(c, s):
                nc.scalar.copy(X1[:, bass.ds(c * C, C), :], x_ring[:, s, :, 0:D]).then_inc(a_xd, 1)

            def lay_out(c, s):
                nc.scalar.copy(di_ring[:, s, :], dst_x[:, bass.ds(c * C + 1, C)])
                nc.scalar.copy(si_ring[:, s, :], src_i[:, bass.ds(c * C, C)]).then_inc(a_idx, 1)

            def chunk_A(c, s, after=True, ahead=True):
                look(c + 1, 0, 1 - s)
                x_T(c, 0)
                if after:
                    deviate(c - 2)
                look(c + 1, 1, 1 - s)
                relu_1(c, 0)
                look(c + 1, 2, 1 - s)
                relu_2(c, 0)
                x_T(c, 1)
                if ahead:
                    lay_out(c + 2, s)
                keep_x(c, s)
                look(c + 1, 3, 1 - s)
                relu_3(c, 0)
                relu_1(c, 1)
                look(c + 1, 4, 1 - s)
                spread_mask(c, 0)
                relu_2(c, 1)
                look(c + 1, 5, 1 - s)
                relu_3(c, 1)
                look(c + 1, 6, 1 - s)

            def deviate(c):
                cols = bass.ds(c * C, C)
                need(act, v_ss, c + 1)
                need(act, v_y1, c)
                nc.scalar.activation(st[:, 6, 0:C], rstd[:, cols], ACT.Sqrt, bias=epsc[:, 0:1]).then_inc(a_sd, 1)

            for u in range(UNITS):
                look(0, u, 0)
            act.wait_ge(s_wts, 16 * WT_DMAS)
            act.wait_ge(v_const, 1)
            chunk_A(0, 0, after=False)
            chunk_A(1, 1, after=False)
            with act.Fori(1, LOOPS - 1) as i:
                chunk_A(i * 2, 0)
                chunk_A(i * 2 + 1, 1)
            chunk_A(2 * LOOPS - 2, 0, ahead=False)
            c = 2 * LOOPS - 1
            x_T(c, 0)
            deviate(c - 2)
            relu_1(c, 0)
            relu_2(c, 0)
            relu_3(c, 0)
            deviate(c - 1)
            x_T(c, 1)
            keep_x(c, 1)
            spread_mask(c, 0)
            relu_1(c, 1)
            relu_2(c, 1)
            relu_3(c, 1)
            deviate(c)
            act.wait_ge(v_jss, 1)
            nc.scalar.activation(j_rstd[:, :], j_rstd[:, :], ACT.Sqrt, bias=epsc[:, 0:1]).then_inc(a_jsd, 1)

            def square_1(k, pn=P, rn=R):
                need(act, v_dxc, k + 1)
                nc.scalar.activation(sqd[0:pn, 0:rn, :], x1d[0:pn, 0:rn, :], ACT.Square).then_inc(a_dsq, 1)

            def deviate_1(k, pn=P, rn=R):
                need(act, v_dss, k + 1)
                deviation(4, rn, pn).then_inc(a_dsd, 1)

            def move_x1T(w0, pn=P, banks=BANKS):
                for b, n in enumerate(banks):
                    need(act, t_dT, w0 + b + 1)
                    need(act, t_dh, w0 + b - 1)
                    m = n * P if pn == P else pn
                    nc.scalar.copy(x1T[:, b % 2, 0:m], x1T_ps[b % 2][:, 0:m]).then_inc(a_dT, 1)

            def square_2(k, pn=P, rn=R):
                need(act, v_dxc2, k + 1)
                need(act, o_od, k)
                nc.scalar.activation(od[0:pn, 0:rn, :], rd[0:pn, 0:rn, :], ACT.Square).then_inc(a_dsq2, 1)

            def deviate_2(k, pn=P, rn=R):
                need(act, v_dss2, k + 1)
                deviation(5, rn, pn).then_inc(a_dsd2, 1)

            def both(i, k, stage):
                spread_mask(i * 2, stage)
                square_2(k - 1)
                square_1(k)
                keep_sums(i * 2, stage)
                spread_mask(i * 2 + 1, stage)
                deviate_1(k)
                deviate_2(k - 1)
                move_x1T(k * 4)
                keep_sums(i * 2 + 1, stage)

            def both_alone(i, stage, k):
                spread_mask(i * 2, stage)
                square_2(k - 1)
                square_1(k)
                keep_sums(i * 2, stage)
                spread_mask(i * 2 + 1, stage)
                deviate_2(k - 1)
                keep_sums(i * 2 + 1, stage)

            square_1(0)
            deviate_1(0)
            move_x1T(0)
            with act.Fori(0, B_BOTH) as i:
                both(i, i + 1, 1)
            both_alone(LOOPS - 1, 1, B_BOTH + 1)
            deviate_1(B_BOTH + 1)
            move_x1T((B_BOTH + 1) * 4)
            act.wait_ge(s_y2, 16 * 2 * LOOPS)
            with act.Fori(0, C_BOTH) as i:
                both(i, i + (B_BOTH + 2), 2)
            c = 2 * C_BOTH
            spread_mask(c, 2)
            square_2(NK - 1)
            square_1(NK, TAILP, TAILR)
            keep_sums(c, 2)
            deviate_1(NK, TAILP, TAILR)
            deviate_2(NK - 1)
            move_x1T(NK * 4, TAILP, [1])
            spread_mask(c + 1, 2)
            keep_sums(c + 1, 2)
            square_2(NK, TAILP, TAILR)
            deviate_2(NK, TAILP, TAILR)

            def z_part(c, s):
                nc.scalar.copy(Z[s][:, :, 0:D], X1[:, bass.ds(c * C, C), :]).then_inc(a_z, 1)

            act.wait_ge(v_const, 3)
            z_part(0, 0)

            def finish(c, s, more=True):
                for b, n in enumerate(FBANKS):
                    need(act, t_ZT, c * 4 + b + 1)
                    need(act, t_hf, c * 4 + b - 1)
                    nc.scalar.copy(ZT[:, b % 2, 0:n * P], ZT_ps[b % 2][:, 0:n * P]).then_inc(a_ZT, 1)
                if more:
                    z_part(c + 1, 1 - s)
                need(act, v_fxc, c + 1)
                nc.scalar.activation(sqf[:, 0:C, :], corr[:, 0:C, :], ACT.Square).then_inc(a_fsq, 1)
                need(act, v_fss, c + 1)
                deviation(7, C).then_inc(a_fsd, 1)

            for c in (2 * LOOPS - 2, 2 * LOOPS - 1):
                spread_mask(c, 2)
                keep_sums(c, 2)
                if c == 2 * LOOPS - 2:
                    finish(0, 0)
                    finish(1, 1)
            with act.Fori(1, LOOPS - 1) as i:
                finish(i * 2, 0)
                finish(i * 2 + 1, 1)
            finish(2 * LOOPS - 2, 0)
            finish(2 * LOOPS - 1, 1, more=False)
            act.wait_ge(t_jz, 1)
            nc.scalar.copy(ZT[:, 0, 0:P], ZT_ps[0][:, 0:P]).then_inc(a_jz, 1)
            act.wait_ge(v_jss, 2)
            nc.scalar.activation(j_rstd[:, :], j_rstd[:, :], ACT.Sqrt, bias=epsc[:, 0:1]).then_inc(a_jsd, 1)

        @block.vector
        def _(dve):
            class Steps:

                def __init__(self, base):
                    self.base, self.n = base, 0

                def done(self, ins):
                    self.n += 1
                    ins.then_inc(v_step, 1)

                def seen(self):
                    need(dve, v_step, self.base + self.n)

                def link(self, ins):
                    self.done(ins)
                    self.seen()

            at = Steps(0)
            link = at.link

            dve.memset(dst_x[:, :], PAD).then_inc(v_pad, 1)
            dve.memset(src_i[:, :], PAD).then_inc(v_pad, 1)
            dve.memset(w[:, :], 0.0).then_inc(v_pad, 1)
            dve.memset(dst_up[:, :], -1).then_inc(v_pad, 1)
            for q in (v_le, v_cnt, v_m, v_y, v_idx, v_di, v_y1, v_y2, v_dxc, v_dx1, v_dh, v_dxc2, v_od, v_z,
                      v_fh, v_fxc, v_o, v_step, v_ss, v_dss, v_dss2, v_fss,
                      v_scan):
                dve.sem_inc(q, OFF)
            dve.memset(x_ring[:, :, :, :], 0.0).then_inc(v_rings, 1)
            dve.memset(y_ring[:, :, :, :], 0.0).then_inc(v_rings, 1)
            dve.memset(w1s[:, :], 0.0).then_inc(v_fill, 1)
            dve.memset(w1b[:, :], 0.0).then_inc(v_fill, 1)
            dve.memset(w2s[:, :, :], 0.0).then_inc(v_fill, 1)
            dve.memset(w3s[:, :, :], 0.0).then_inc(v_fill, 1)
            dve.memset(w4s[:, :], 0.0).then_inc(v_fill, 1)
            dve.memset(wd[:, :], 0.0).then_inc(v_fill, 1)
            dve.memset(wd2[:, :], 0.0).then_inc(v_fill, 1)
            dve.memset(wf[:, :], 0.0).then_inc(v_fill, 1)
            dve.memset(epsc[:, :], D * EPS).then_inc(v_fill, 1)
            dve.memset(ones[:, :], 1.0)
            dve.memset(zeros[:, :], 0.0)
            dve.memset(onerow[:, :], 1.0)
            dve.memset(src4[:, :], 0.0)
            dve.memset(sc_out[:, :, :], 0.0)
            dve.memset(mk[:, :, :], 0.0).then_inc(v_const, 1)
            dve.memset(carT[:, :], 0.0)
            dve.memset(b_parts[:, :], 0.0)
            link(dve.memset(tails[:, :], 0.0))

            dve.wait_ge(s_nodes, 16 * NODE_DMAS)
            dve.wait_ge(s_edges, 16 * EDGE_DMAS)
            dve.tensor_scalar(dst1[:, :], dst_x[:, :], 1.0, None, ALU.add)
            dve.tensor_scalar(src4[:, 0:T], src_i[:, :], 1.0, 0.25, ALU.add, ALU.mult)
            link(dve.tensor_scalar(tmp[:, :], dst_up[:, :], 1.0, None, ALU.add))
            dve.wait_ge(p_id, 2)
            dve.tensor_copy(ident16[:, :], ident[:, :])
            dve.tensor_scalar(diag[:, :], ident[:, :], dst1[:, 1:2], 0.25, ALU.mult, ALU.mult).then_inc(v_diag, 1)
            link(dve.tensor_tensor(d_diff[:, :], dst1[:, 1:T + 1], tmp[:, :], ALU.subtract))
            link(dve.tensor_scalar(d_delta[:, 0, :], d_diff[:, :], 0.25, None, ALU.mult))
            dve.scalar_tensor_tensor(out=d_delta[:, 1, :], in0=d_diff[:, :], scalar=0.25, in1=d_delta[:, 0, :],
                                     op0=ALU.mult, op1=ALU.subtract)
            dve.tensor_tensor(cont[:, :], dst1[:, 0:T], dst1[:, 1:T + 1], ALU.is_equal)
            link(dve.tensor_tensor(last[:, :], dst1[:, 1:T + 1], dst1[:, 2:T + 2], ALU.not_equal))
            dve.tensor_tensor_scan(pre[:, :], cont[:, :], zeros[:, :], 1.0, ALU.mult, ALU.add)
            dve.tensor_tensor_scan(cnt[:, :], cont[:, :], ones[:, :], 0.0, ALU.mult, ALU.add)
            link(dve.tensor_tensor_scan(deg[:, :], cont[:, :], w[:, :], 0.0, ALU.mult, ALU.add))

            def send_tails(k):
                if k == 0:
                    dve.tensor_copy(tails[:, 0:1], cnt[:, T - 1:T])
                    dve.tensor_copy(tails[:, 1:2], deg[:, T - 1:T])
                    dve.tensor_copy(spans[:, :], pre[:, T - 1:T].broadcast_to([P, D])).then_inc(v_tail, 1)
                else:
                    dve.tensor_copy(tails[:, :], sc_out[:, :, C]).then_inc(v_tail, 1)

            def carry(k, at):
                carry_scan(k, at)
                carry_back(k, at)

            def carry_scan(k, at):
                dve.wait_ge(t_tail, k + 1)
                if k == 0:
                    at.done(dve.tensor_copy(spanT[:, :], car_ps[0:D, P:2 * P]))
                at.link(dve.tensor_copy(tailT[:, :], car_ps[0:D, 0:P]))
                dve.tensor_tensor_scan(carT[:, 1:P], spanT[:, 0:P - 1], tailT[:, 0:P - 1], 0.0,
                                       ALU.mult, ALU.add).then_inc(v_ct, 1)

            def carry_back(k, at):
                dve.wait_ge(t_ct, k + 1)
                at.link(dve.tensor_copy(car[:, k, :], car_ps[:, 2 * P:2 * P + D]))

            dve.wait_ge(t_d0, 1)
            link(dve.tensor_copy(d_first[:, :], dq_ps[:, 0:P]))
            send_tails(0)
            carry(0, at)
            dve.scalar_tensor_tensor(out=cnt[:, :], in0=pre[:, :], scalar=car[:, 0, 0:1], in1=cnt[:, :],
                                     op0=ALU.mult, op1=ALU.add)
            link(dve.scalar_tensor_tensor(out=deg[:, :], in0=pre[:, :], scalar=car[:, 0, 1:2], in1=deg[:, :],
                                          op0=ALU.mult, op1=ALU.add))
            dve.reciprocal(rcnt[:, :], cnt[:, :])
            dve.tensor_scalar(dinv[:, :], deg[:, :], 1e-12, None, ALU.max).then_inc(v_deg, 1)
            dve.tensor_scalar(tmp[:, :], deg[:, :], 0.0, None, ALU.is_gt)
            dve.wait_ge(a_deg, 1)
            link(dve.reciprocal(dinv[:, :], dinv[:, :]))
            dve.tensor_copy(joint[:, T - 1:T], pre[:, T - 1:T])
            dve.tensor_tensor(joint[:, 0:T - 1], pre[:, 0:T - 1], pre[:, 1:T], ALU.subtract)
            link(dve.tensor_tensor(dinv[:, :], dinv[:, :], tmp[:, :], ALU.mult))
            dve.tensor_scalar(ndinv[:, :], dinv[:, :], -1.0, None, ALU.mult)
            dve.tensor_scalar(n2dinv[:, :], dinv[:, :], -2.0, None, ALU.mult)
            link(dve.scalar_tensor_tensor(out=ndinv2[:, :], in0=dinv[:, :], scalar=-1.0, in1=dinv[:, :],
                                          op0=ALU.mult, op1=ALU.mult))

            def compare(c, u, s):
                U, b = c * UNITS + u, (s + u) % 2
                need(dve, t_leT, U - 1)
                for j in range(2):
                    t = c * C + (2 * u + j)
                    ins = dve.tensor_scalar(le[:, b, j, :], d_first[:, :], src4[:, bass.ds(t, 1)], 0.0,
                                            ALU.is_le, ALU.add, accum_out=above[:, bass.ds(t, 1)])
                ins.then_inc(v_le, 1)

            def count(c, u):
                U = c * UNITS + u
                need(dve, t_dq, U + 1)
                need(dve, v_cnt, U)
                for j in range(2):
                    t = c * C + (2 * u + j)
                    dve.tensor_scalar(hits[:, 2 * j, :], dq_ps[:, j * T:(j + 1) * T], src4[:, bass.ds(t, 1)], 0.0,
                                      ALU.is_le, ALU.add, accum_out=below[:, bass.ds(t, 1)])
                    ins = dve.tensor_scalar(hits[:, 2 * j + 1, :], dq_ps[:, j * T:(j + 1) * T],
                                            src4[:, bass.ds(t, 1)], 0.0, ALU.is_equal, ALU.add, accum_out=same[:, bass.ds(t, 1)])
                ins.then_inc(v_cnt, 1)

            def scan(at, c, stage):
                g = c + stage * 2 * LOOPS
                at.link(dve.tensor_copy(sc_in[:, :, 0], sc_out[:, :, C]))
                need(dve, a_mk, g + 1)
                if stage:
                    need(dve, a_S, g - 2 * LOOPS)
                dve.tensor_tensor_scan(sc_out[:, :, :].rearrange("p f t -> p (f t)"),
                                       mk[:, :, :].rearrange("p f t -> p (f t)"),
                                       sc_in[:, :, :].rearrange("p f t -> p (f t)"), 0.0, ALU.mult,
                                       ALU.add).then_inc(v_scan, 1)
                need(dve, v_scan, g + 1)

            sums = sc_out[:, :, 1:C + 1].rearrange("p f t -> p t f")

            compare(0, 0, 0)
            compare(0, 1, 0)
            for u in range(UNITS):
                count(0, u)
                compare(0, u + 2, 0)

            dve.wait_ge(s_wts, 16 * WT_DMAS)
            dve.tensor_tensor(w1s[:, :], w1s[:, :], w1b[:, :], ALU.subtract)
            dve.tensor_tensor(wd[:, :], wd[:, :], wd2[:, :], ALU.subtract)
            dve.tensor_copy(b_parts[0:1, :], brow[0:1, :])
            link(dve.tensor_copy(b_near[:, :], brow[:, :]))
            link(dve.tensor_tensor(brow[:, :], brow[:, :], b_near[:, :], ALU.subtract))
            dve.tensor_copy(b_parts[32:33, :], brow[32:33, :])
            link(dve.tensor_copy(b_near[:, :], brow[:, :]))
            link(dve.tensor_tensor(brow[:, :], brow[:, :], b_near[:, :], ALU.subtract))
            dve.tensor_copy(b_parts[64:65, :], brow[64:65, :])
            dve.tensor_tensor(wf[0:D, :], wf[0:D, :], wf2[:, :], ALU.subtract).then_inc(v_wts, 1)

            link(dve.tensor_scalar(tmp[:, :], dst1[:, 1:T + 1], float(BIG - 1), None, ALU.add))
            link(dve.scalar_tensor_tensor(out=tmp[:, :], in0=last[:, :], scalar=-float(BIG), in1=tmp[:, :],
                                          op0=ALU.mult, op1=ALU.add))
            link(dve.scalar_tensor_tensor(out=scat_i[:, :], in0=joint[:, :], scalar=float(BIG), in1=tmp[:, :],
                                          op0=ALU.mult, op1=ALU.add))
            link(dve.tensor_tensor(j_hits[:, :], joint[:, :], tmp[:, :], ALU.mult))
            link(dve.tensor_reduce(tmp[:, 4:5], j_hits[:, :], AX, ALU.add))
            dve.memset(j_sums[:, :, :], 0.0)
            link(dve.memset(j_old[:, :], 0.0))
            dve.memset(j_row[:, :], 0.0)
            for k, a in enumerate((rcnt, dinv, ndinv2)):
                link(dve.tensor_tensor(j_hits[:, :], joint[:, :], a[:, :], ALU.mult))
                link(dve.tensor_reduce(j_scal[:, k, :], j_hits[:, :], AX, ALU.add))
            link(dve.tensor_tensor_scan(j_hits[:, 0:P], ones[:, 0:P], ones[:, 0:P], -1.0, ALU.mult, ALU.add))
            link(dve.tensor_tensor(j_hits[:, 0:P], j_hits[:, 0:P], ident[:, :], ALU.mult))
            link(dve.tensor_reduce(tmp[:, 0:1], j_hits[:, 0:P], AX, ALU.add))
            link(dve.tensor_reduce(tmp[:, 1:2], pre[:, :], AX, ALU.add))
            dve.tensor_scalar(tmp[:, 2:3], tmp[:, 1:2], 0.0, float(BIG), ALU.is_equal, ALU.mult)
            link(dve.tensor_scalar(tmp[:, 3:4], tmp[:, 0:1], float(T), -1.0, ALU.mult, ALU.add))
            link(dve.tensor_tensor(tmp[:, 3:4], tmp[:, 3:4], tmp[:, 1:2], ALU.add))
            dve.tensor_tensor(j_scat[:, :], tmp[:, 4:5], tmp[:, 2:3], ALU.add)
            link(dve.tensor_tensor(j_i[:, :], tmp[:, 3:4], tmp[:, 2:3], ALU.add))

            def norm_sum(at, rows, k, n, pn=P):
                at.link(dve.tensor_reduce(st[0:pn, k, 0:n], rows, AX, ALU.add))

            def centre(o, rows, k, n, pn=P):
                return dve.scalar_tensor_tensor(out=o, in0=over_f(st[0:pn, k, 0:n], n), scalar=-1.0 / D, in1=rows,
                                                op0=ALU.mult, op1=ALU.add)

            def norm_squares(sq, k, n, pn=P):
                return dve.tensor_reduce(st[0:pn, k, 0:n], sq, AX, ALU.add)

            def scaled(o, rows, k, n, pn=P):
                return dve.scalar_tensor_tensor(out=o, in0=rows, scalar=RT32, in1=over_f(st[0:pn, k, 0:n], n),
                                                op0=ALU.mult, op1=ALU.mult)

            def invert(at, k, n, pn=P):
                at.link(dve.reciprocal(st[0:pn, k, 0:n], st[0:pn, k, 0:n]))

            def weigh(at, c, s, i, stage, ahead=True):
                dve.wait_ge(s_gy[s], (i + (1 + (stage - 1) * LOOPS)) * (16 * C))
                if ahead:
                    dve.tensor_copy(si_ring[:, s, :], slot_i[:, bass.ds((c + 2) * C, C)]).then_inc(v_idx, 1)
                need(dve, v_scan, c + stage * 2 * LOOPS)
                dve.tensor_tensor(sc_in[:, :, 1:C + 1], y_ring[:, s, :, :].rearrange("p t f -> p f t"),
                                  w_eff[:, bass.ds(c * C, C)].rearrange("p (o t) -> p o t", o=1)
                                  .broadcast_to([P, D, C]), ALU.mult).then_inc(v_y, 1)
                scan(at, c, stage)
                if stage == 1:
                    cols = bass.ds(c * C, C)
                    dve.tensor_tensor(T1[:, cols, :], sums, over_f(ndinv2[:, cols], C), ALU.mult).then_inc(v_y2, 1)

            def dense_centre(at, k, pn=P, rn=R):
                dve.wait_ge(s_xin, (k + 1) * 16)
                norm_sum(at, xin[0:pn, 0:rn, :], 3, rn, pn)
                centre(x1d[0:pn, 0:rn, :], xin[0:pn, 0:rn, :], 3, rn, pn).then_inc(v_dxc, 1)

            def dense_squares_1(k, pn=P, rn=R):
                need(dve, a_dsq, k + 1)
                norm_squares(sqd[0:pn, 0:rn, :], 4, rn, pn).then_inc(v_dss, 1)

            def dense_x1(at, k, pn=P, rn=R):
                need(dve, a_dsd, k + 1)
                invert(at, 4, rn, pn)
                scaled(x1d[0:pn, 0:rn, :], x1d[0:pn, 0:rn, :], 4, rn, pn).then_inc(v_dx1, 1)

            def dense_sum(at, k, w0, pn=P, rn=R, banks=BANKS):
                need(dve, v_dx1, k + 1)
                need(dve, v_od, k)
                for b, n in enumerate(banks):
                    need(dve, t_dh, w0 + b + 1)
                    r = 4 * sum(banks[0:b])
                    rows = x1d[0:pn, r:r + 4 * n, :]
                    dve.scalar_tensor_tensor(
                        out=rd[0:pn, r:r + 4 * n, :].rearrange("p a b -> p (a b)"),
                        in0=hd_ps[b % 2][0:pn, 0:n * P], scalar=0.0,
                        in1=rows.rearrange("p a b -> p (a b)"), op0=ALU.max, op1=ALU.add).then_inc(v_dh, 1)
                need(dve, v_dh, w0 + len(banks))
                norm_sum(at, rd[0:pn, 0:rn, :], 2, rn, pn)
                centre(rd[0:pn, 0:rn, :], rd[0:pn, 0:rn, :], 2, rn, pn).then_inc(v_dxc2, 1)

            def dense_squares_2(k, pn=P, rn=R):
                need(dve, a_dsq2, k + 1)
                norm_squares(od[0:pn, 0:rn, :], 5, rn, pn).then_inc(v_dss2, 1)

            def dense_out(at, k, pn=P, rn=R):
                need(dve, a_dsd2, k + 1)
                invert(at, 5, rn, pn)
                scaled(od[0:pn, 0:rn, :], rd[0:pn, 0:rn, :], 5, rn, pn).then_inc(v_od, 1)

            def both(at, i, k, stage, more=True):
                weigh(at, i * 2, 0, i, stage)
                dense_squares_1(k)
                dense_squares_2(k - 1)
                dense_x1(at, k)
                dense_out(at, k - 1)
                weigh(at, i * 2 + 1, 1, i, stage)
                dense_sum(at, k, k * 4)
                if more:
                    dense_centre(at, k + 1)
                else:
                    dense_centre(at, k + 1, TAILP, TAILR)

            def dense_between(at, k):
                dense_squares_1(k)
                dense_x1(at, k)
                dense_sum(at, k, k * 4)
                dense_centre(at, k + 1)

            def sum_messages(c, at):
                need(dve, t_m, c * 2 + 2)
                need(dve, v_scan, c)
                dve.tensor_tensor(sc_in[:, :, 1:C + 1],
                                  m_ps[:, 0:C * D].rearrange("p (t f) -> p f t", f=D),
                                  b4r[:, :].rearrange("p (f o) -> p f o", o=1).broadcast_to([P, D, C]),
                                  ALU.add).then_inc(v_m, 1)
                scan(at, c, 0)

            def add_mean(c, at):
                cols = bass.ds(c * C, C)
                cr = corr[:, 0:C, :]
                at.link(dve.tensor_tensor(cr, sums, over_f(rcnt[:, cols], C), ALU.mult))
                need(dve, a_xd, c + 1)
                at.link(dve.tensor_tensor(cr, X1[:, cols, :], cr, ALU.add))

            def centre_x1(c, at):
                cr = corr[:, 0:C, :]
                at.link(dve.tensor_reduce(st[:, 0, 0:C], cr, AX, ALU.add))
                at.link(dve.scalar_tensor_tensor(out=X1[:, bass.ds(c * C, C), :], in0=over_f(st[:, 0, 0:C], C),
                                                 scalar=-1.0 / D, in1=cr, op0=ALU.mult, op1=ALU.add))

            def square_x1(c, at):
                cols = bass.ds(c * C, C)
                sq = corr[:, C:C2, :]
                at.link(dve.tensor_tensor(sq, X1[:, cols, :], X1[:, cols, :], ALU.mult))
                dve.tensor_reduce(rstd[:, cols], sq, AX, ALU.add).then_inc(v_ss, 1)

            def pick_old_row(c, at):
                cols = bass.ds(c * C, C)
                at.link(dve.tensor_tensor(corr[:, 0:C, :], X1[:, cols, :], over_f(joint[:, cols], C), ALU.mult))

            def pick_old_sum(at):
                cr = corr[:, 0:C, :]
                at.link(dve.tensor_reduce(j_part[:, :], cr.rearrange("p t f -> p f t"), AX, ALU.add))
                at.done(dve.tensor_tensor(j_old[:, :], j_old[:, :], j_part[:, :], ALU.add))

            def make_y1(c, at):
                cols = bass.ds(c * C, C)
                need(dve, a_sd, c + 1)
                at.link(dve.reciprocal(st[:, 6, 0:C], st[:, 6, 0:C]))
                at.done(dve.tensor_scalar(rstd[:, cols], st[:, 6, 0:C], 1.0, None, ALU.mult))
                at.link(scaled(X1[:, cols, :], X1[:, cols, :], 6, C))
                dve.tensor_tensor(T1[:, cols, :], X1[:, cols, :], over_f(dinv[:, cols], C),
                                  ALU.mult).then_inc(v_y1, 1)

            def look_A(c, u, s):
                count(c, u)
                compare(c, u + 2, s)

            def chunk_A(c, s, at, after=True, after_2=True):
                look_A(c + 1, 0, 1 - s)
                if after:
                    sum_messages(c - 1, at)
                look_A(c + 1, 1, 1 - s)
                if after:
                    add_mean(c - 1, at)
                look_A(c + 1, 2, 1 - s)
                if after:
                    centre_x1(c - 1, at)
                look_A(c + 1, 3, 1 - s)
                if after:
                    square_x1(c - 1, at)
                look_A(c + 1, 4, 1 - s)
                if after:
                    pick_old_row(c - 1, at)
                    pick_old_sum(at)
                look_A(c + 1, 5, 1 - s)
                if after_2:
                    make_y1(c - 2, at)
                look_A(c + 1, 6, 1 - s)

            base, K_A = at.n, 24
            at = Steps(base)
            chunk_A(0, 0, at, after=False, after_2=False)
            chunk_A(1, 1, at, after_2=False)
            base += at.n
            with dve.Fori(1, LOOPS - 1) as i:
                at = Steps((i - 1) * K_A + base)
                chunk_A(i * 2, 0, at)
                chunk_A(i * 2 + 1, 1, at)
                assert at.n == K_A, at.n
            base += K_A * (LOOPS - 2)
            at = Steps(base)
            LAST = 2 * LOOPS - 1
            chunk_A(LAST - 1, 0, at)
            sum_messages(LAST - 1, at)
            add_mean(LAST - 1, at)
            centre_x1(LAST - 1, at)
            square_x1(LAST - 1, at)
            pick_old_row(LAST - 1, at)
            pick_old_sum(at)
            make_y1(LAST - 2, at)
            need(dve, v_cnt, 2 * LOOPS * UNITS)
            at.link(dve.tensor_scalar(tmp[:, :], same[:, :], 0.0, None, ALU.is_gt))
            at.link(dve.scalar_tensor_tensor(out=below[:, :], in0=above[:, 0:T], scalar=float(T), in1=below[:, :],
                                             op0=ALU.mult, op1=ALU.add))
            at.done(dve.tensor_tensor(w_eff[:, :], w[:, :], tmp[:, :], ALU.mult))
            at.link(dve.tensor_scalar(below[:, :], below[:, :], float(BIG - T - 1), None, ALU.add))
            dve.scalar_tensor_tensor(out=slot_i[:, :], in0=tmp[:, :], scalar=-float(BIG), in1=below[:, :],
                                     op0=ALU.mult, op1=ALU.add).then_inc(v_slot, 1)
            dense_centre(at, 0)
            make_y1(LAST - 1, at)
            sum_messages(LAST, at)
            send_tails(1)
            add_mean(LAST, at)
            carry_scan(1, at)
            centre_x1(LAST, at)
            carry_back(1, at)
            square_x1(LAST, at)
            at.link(dve.tensor_reduce(st[:, 1, 0:1], car[:, 1, :], AX, ALU.add))
            at.link(dve.scalar_tensor_tensor(out=carc[:, :], in0=st[:, 1, 0:1].broadcast_to([P, D]),
                                             scalar=-1.0 / D, in1=car[:, 1, :], op0=ALU.mult, op1=ALU.add))
            pick_old_row(LAST, at)
            make_y1(LAST, at)
            pick_old_sum(at)
            at.seen()
            at.link(dve.scalar_tensor_tensor(out=j_new[:, :], in0=carc[:, :], scalar=j_scal[:, 0, :],
                                             in1=j_old[:, :], op0=ALU.mult, op1=ALU.add))
            at.link(dve.tensor_tensor(j_sq[:, :], j_new[:, :], j_new[:, :], ALU.mult))
            dve.tensor_reduce(j_rstd[:, :], j_sq[:, :], AX, ALU.add).then_inc(v_jss, 1)
            dve.wait_ge(a_jsd, 1)
            at.link(dve.reciprocal(j_rstd[:, :], j_rstd[:, :]))
            at.link(dve.tensor_scalar(j_new[:, :], j_new[:, :], j_rstd[:, 0:1], RT32, ALU.mult, ALU.mult))
            dve.tensor_scalar(j_y1[:, :], j_new[:, :], j_scal[:, 1, :], None, ALU.mult).then_inc(v_j1, 1)
            at.link(dve.memset(sc_out[:, :, C], 0.0))
            base += at.n

            at = Steps(base)
            dense_between(at, 0)
            base += at.n
            K_B = 6
            with dve.Fori(0, B_BOTH) as i:
                at = Steps(i * K_B + base)
                both(at, i, i + 1, 1)
                assert at.n == K_B, at.n
            base += K_B * B_BOTH
            at = Steps(base)
            weigh(at, 2 * LOOPS - 2, 0, LOOPS - 1, 1, ahead=False)
            dense_squares_2(B_BOTH)
            dense_out(at, B_BOTH)
            weigh(at, 2 * LOOPS - 1, 1, LOOPS - 1, 1, ahead=False)
            send_tails(2)
            carry(2, at)
            at.done(dve.tensor_scalar(j_sq[:, :], car[:, 2, :], j_scal[:, 2, :], None, ALU.mult))
            at.seen()
            dve.wait_ge(s_jg, 16)
            dve.tensor_tensor(j_y2[:, :], j_row[:, :], j_sq[:, :], ALU.add).then_inc(v_j2, 1)
            need(dve, a_S, 2 * LOOPS)
            at.link(dve.memset(sc_out[:, :, C], 0.0))

            dense_between(at, B_BOTH + 1)
            base += at.n
            K_C = 6
            with dve.Fori(0, C_BOTH - 1) as i:
                at = Steps(i * K_C + base)
                both(at, i, i + (B_BOTH + 2), 2)
                assert at.n == K_C, at.n
            base += K_C * (C_BOTH - 1)
            at = Steps(base)
            both(at, C_BOTH - 1, NK - 1, 2, more=False)
            weigh(at, 2 * C_BOTH, 0, C_BOTH, 2)
            dense_squares_1(NK, TAILP, TAILR)
            dense_squares_2(NK - 1)
            dense_x1(at, NK, TAILP, TAILR)
            dense_out(at, NK - 1)
            weigh(at, 2 * C_BOTH + 1, 1, C_BOTH, 2)
            dense_sum(at, NK, NK * 4, TAILP, TAILR, [1])
            dense_squares_2(NK, TAILP, TAILR)
            dense_out(at, NK, TAILP, TAILR)
            need(dve, v_od, NK + 1)
            for z in Z:
                at.link(dve.memset(z[:, :, 3 * D:4 * D], 0.0))
                dve.memset(z[:, :, 3 * D:3 * D + 1], 1.0).then_inc(v_const, 1)

            def z_rows(at, c, s):
                cols = bass.ds(c * C, C)
                need(dve, a_S, c + (1 + 2 * LOOPS))
                at.done(dve.tensor_tensor(Z[s][:, :, D:2 * D], S[:, cols, :], over_f(ndinv[:, cols], C), ALU.mult))
                dve.tensor_tensor(Z[s][:, :, 2 * D:3 * D], T1[:, cols, :], over_f(n2dinv[:, cols], C),
                                  ALU.mult).then_inc(v_z, 1)

            def pick_joints(at, c):
                cols = bass.ds(c * C, C)
                picked = (cz[:, :, :], sqf[:, C:C2, :])
                at.done(dve.tensor_tensor(picked[0], S[:, cols, :], over_f(joint[:, cols], C), ALU.mult))
                at.link(dve.tensor_tensor(picked[1], T1[:, cols, :], over_f(joint[:, cols], C), ALU.mult))
                for k in range(2):
                    ins = dve.tensor_reduce(j_parts[:, k, :], picked[k].rearrange("p t f -> p f t"), AX, ALU.add)
                    at.done(ins)
                at.seen()
                at.link(dve.tensor_tensor(j_sums[:, :, :], j_sums[:, :, :], j_parts[:, :, :], ALU.add))

            def finish(at, c, s, more=True):
                if more:
                    z_rows(at, c + 1, 1 - s)
                pick_joints(at, c)
                cols = bass.ds(c * C, C)
                cr = corr[:, 0:C, :]
                need(dve, v_o, c)
                need(dve, t_hf, c * 4 + 4)
                dve.scalar_tensor_tensor(out=cr, in0=hf_ps[:, 0:C * D].rearrange("p (t f) -> p t f", f=D),
                                         scalar=0.0, in1=X1[:, cols, :], op0=ALU.max,
                                         op1=ALU.add).then_inc(v_fh, 1)
                need(dve, v_fh, c + 1)
                norm_sum(at, cr, 6, C)
                centre(cr, cr, 6, C).then_inc(v_fxc, 1)
                need(dve, a_fsq, c + 1)
                norm_squares(sqf[:, 0:C, :], 7, C).then_inc(v_fss, 1)
                need(dve, a_fsd, c + 1)
                invert(at, 7, C)
                need(dve, o_sc, c - 1)
                dve.tensor_scalar(di_ring[:, s, :], scat_i[:, cols], 0.0, None, ALU.add).then_inc(v_di, 1)
                scaled(o_ring[:, s, :, :], cr, 7, C).then_inc(v_o, 1)

            z_rows(at, 0, 0)
            weigh(at, 2 * LOOPS - 2, 0, LOOPS - 1, 2, ahead=False)
            finish(at, 0, 0)
            finish(at, 1, 1)
            weigh(at, 2 * LOOPS - 1, 1, LOOPS - 1, 2, ahead=False)
            send_tails(3)
            carry(3, at)
            base += at.n
            K_F = 16
            with dve.Fori(1, LOOPS - 1) as i:
                at = Steps((i - 1) * K_F + base)
                finish(at, i * 2, 0)
                finish(at, i * 2 + 1, 1)
                assert at.n == K_F, at.n
            at = Steps(base + K_F * (LOOPS - 2))
            finish(at, 2 * LOOPS - 2, 0)
            finish(at, 2 * LOOPS - 1, 1, more=False)
            zj = Z[0][:, 0, :]
            at.done(dve.tensor_tensor(j_sums[:, :, :], j_sums[:, :, :], car[:, 2:4, :], ALU.add))
            at.link(dve.tensor_copy(zj[:, 0:D], j_new[:, :]))
            at.done(dve.tensor_scalar(zj[:, D:2 * D], j_sums[:, 0, :], j_scal[:, 1, :], -1.0, ALU.mult, ALU.mult))
            dve.tensor_scalar(zj[:, 2 * D:3 * D], j_sums[:, 1, :], j_scal[:, 1, :], -2.0, ALU.mult,
                              ALU.mult).then_inc(v_jz, 1)
            dve.wait_ge(t_jh, 1)
            at.link(dve.scalar_tensor_tensor(out=j_new[:, :], in0=hf_ps[:, 0:D], scalar=0.0, in1=j_new[:, :],
                                             op0=ALU.max, op1=ALU.add))
            at.link(dve.tensor_reduce(st[:, 1, 0:1], j_new[:, :], AX, ALU.add))
            at.link(dve.scalar_tensor_tensor(out=j_new[:, :], in0=st[:, 1, 0:1].broadcast_to([P, D]),
                                             scalar=-1.0 / D, in1=j_new[:, :], op0=ALU.mult, op1=ALU.add))
            at.link(dve.tensor_tensor(j_sq[:, :], j_new[:, :], j_new[:, :], ALU.mult))
            dve.tensor_reduce(j_rstd[:, :], j_sq[:, :], AX, ALU.add).then_inc(v_jss, 1)
            dve.wait_ge(a_jsd, 2)
            at.link(dve.reciprocal(j_rstd[:, :], j_rstd[:, :]))
            dve.tensor_scalar(j_out[:, :], j_new[:, :], j_rstd[:, 0:1], RT32, ALU.mult, ALU.mult).then_inc(v_jo, 1)


_INS = ["x", "src", "dst", "edge_weight", "L0_gnn_W1", "L0_gnn_b1", "L0_gnn_W2", "L0_gnn_b2",
        "L0_gnn_W3", "L0_gnn_b3", "L0_gnn_W4", "L0_gnn_b4", "L1_gnn_W", "L1_gnn_b"]


def kernel(**inputs):
    import numpy as _np
    import concourse.bacc as _bacc
    from concourse import mybir as _mybir
    from concourse.bass_utils import run_bass_kernel_spmd as _run

    nc = _bacc.Bacc("TRN2", target_bir_lowering=False, num_devices=1)
    arrays, args = {}, []
    for name in _INS:
        a = _np.ascontiguousarray(inputs[name])
        arrays[f"in_{name}_dram"] = a
        args.append(nc.dram_tensor(f"in_{name}_dram", a.shape, _mybir.dt.from_np(a.dtype), kind="ExternalInput").ap())
    shape = inputs["x"].shape
    o = nc.dram_tensor("out_0_dram", shape, _mybir.dt.float32, kind="ExternalOutput").ap()
    build(nc, *args, o)
    r = _run(nc, [arrays], core_ids=[0])
    return r.results[0]["out_0_dram"]
```
